# Optimizing a Trainium2 kernel written in Bass

```python
import numpy as np
import jax
import jax.numpy as jnp

def _softmax(x, axis=-1):
    return jax.nn.softmax(x, axis=axis)

def _gelu(x):
    return jax.nn.gelu(x, approximate=True)

def _silu(x):
    return jax.nn.silu(x)

def _sigmoid(x):
    return jax.nn.sigmoid(x)

def _layernorm(x, axis=-1, eps=1e-05):
    m = jnp.mean(x, axis=axis, keepdims=True)
    v = jnp.var(x, axis=axis, keepdims=True)
    return (x - m) / jnp.sqrt(v + eps)

def _scatter_add(tgt, idx, src, axis=0):
    return tgt.at[idx].add(src)

def _segment_sum(src, seg, n):
    return jax.ops.segment_sum(src, seg, n)
kernel_name = 'mk_lm_tower_d2_tok_ids256_r4_ffdecf'

def setup_inputs(seed: int=0):
    np.random.seed(seed)
    _w = jnp.asarray

    def _rec_inputs():
        import jax
        import jax.numpy as jnp
        _rk = jax.random.key(seed)
        x = jax.random.randint(jax.random.fold_in(_rk, 1), (8, 1024), 0, 256, jnp.int32)
        return x
    x = _rec_inputs()

    def _L0_tok_setup():
        import jax, jax.numpy as jnp
        import numpy as np
        VOCAB = 256
        EMBED_DIM = 128
        OUT_FEATS = 64
        CTX = 2
        GROUPS = OUT_FEATS // 4
        BLANK_ID = 0
        key = jax.random.key(seed)
        k1, k2, k3, k4, k5 = jax.random.split(key, 5)
        y = jax.random.randint(k1, (64, 256), 0, VOCAB, dtype=jnp.int64)
        embed_table = jax.random.normal(k2, (VOCAB, EMBED_DIM), dtype=jnp.float32) * 0.02
        conv_w = jax.random.normal(k3, (EMBED_DIM, EMBED_DIM // GROUPS, CTX), dtype=jnp.float32) * 0.1
        proj_w = jax.random.normal(k4, (OUT_FEATS, EMBED_DIM), dtype=jnp.float32) * 0.05
        proj_b = jax.random.normal(k5, (OUT_FEATS,), dtype=jnp.float32) * 0.01
        return {'y': y, 'embed_table': embed_table, 'conv_w': conv_w, 'proj_w': proj_w, 'proj_b': proj_b}
    _L0_tok_all = _L0_tok_setup()
    _L0_tok_in = {k: v for k, v in _L0_tok_all.items() if k in ('embed_table', 'conv_w', 'proj_w', 'proj_b')}
    del _L0_tok_all

    def _L0_attn_setup():
        import jax, jax.numpy as jnp
        import numpy as np
        B, S, I, H, O = (64, 128, 64, 256, 64)

        def _rnn_layer(inp, W_ih, W_hh, b_ih, b_hh):
            pre = jnp.einsum('bsi,hi->bsh', inp, W_ih) + (b_ih + b_hh)
            h0 = jnp.zeros((inp.shape[0], W_hh.shape[0]), dtype=inp.dtype)

            def step(h, p_t):
                h = jnp.tanh(p_t + h @ W_hh.T)
                return (h, h)
            _, hs = jax.lax.scan(step, h0, jnp.swapaxes(pre, 0, 1))
            return jnp.swapaxes(hs, 0, 1)
        key = jax.random.key(seed)
        ks = jax.random.split(key, 12)
        s_in = 1.0 / np.sqrt(H)
        inp = {'x': jax.random.normal(ks[0], (B, S, I), dtype=jnp.float32), 'W_ih_0': jax.random.uniform(ks[1], (H, I), jnp.float32, -s_in, s_in), 'W_hh_0': jax.random.uniform(ks[2], (H, H), jnp.float32, -s_in, s_in), 'b_ih_0': jax.random.uniform(ks[3], (H,), jnp.float32, -s_in, s_in), 'b_hh_0': jax.random.uniform(ks[4], (H,), jnp.float32, -s_in, s_in), 'W_ih_1': jax.random.uniform(ks[5], (H, H), jnp.float32, -s_in, s_in), 'W_hh_1': jax.random.uniform(ks[6], (H, H), jnp.float32, -s_in, s_in), 'b_ih_1': jax.random.uniform(ks[7], (H,), jnp.float32, -s_in, s_in), 'b_hh_1': jax.random.uniform(ks[8], (H,), jnp.float32, -s_in, s_in), 'fc_w': jax.random.uniform(ks[9], (O, H), jnp.float32, -s_in, s_in), 'fc_b': jax.random.uniform(ks[10], (O,), jnp.float32, -s_in, s_in)}
        return inp
    _L0_attn_all = _L0_attn_setup()
    _L0_attn_in = {k: v for k, v in _L0_attn_all.items() if k in ('W_ih_0', 'W_hh_0', 'b_ih_0', 'b_hh_0', 'W_ih_1', 'W_hh_1', 'b_ih_1', 'b_hh_1', 'fc_w', 'fc_b')}
    del _L0_attn_all

    def _L0_ffn_setup():
        import jax, jax.numpy as jnp
        import numpy as np
        B, S, D = (8, 1024, 64)
        H = 4 * D
        CAPACITY = 0.5
        key = jax.random.key(seed)
        ks = jax.random.split(key, 6)
        x = jax.random.normal(ks[0], (B, S, D), dtype=jnp.float32)
        attention_mask = jnp.zeros((B, 1, 1, S), dtype=jnp.float32)
        wr = jax.random.normal(ks[1], (D, 1), dtype=jnp.float32) * 0.02
        br = jnp.zeros((1,), dtype=jnp.float32)
        w1 = jax.random.normal(ks[2], (D, H), dtype=jnp.float32) * 0.02
        b1 = jnp.zeros((H,), dtype=jnp.float32)
        w2 = jax.random.normal(ks[3], (H, D), dtype=jnp.float32) * 0.02
        b2 = jnp.zeros((D,), dtype=jnp.float32)
        return {'x': x, 'attention_mask': attention_mask, 'wr': wr, 'br': br, 'w1': w1, 'b1': b1, 'w2': w2, 'b2': b2}
    _L0_ffn_all = _L0_ffn_setup()
    _L0_ffn_in = {k: v for k, v in _L0_ffn_all.items() if k in ('attention_mask', 'wr', 'br', 'w1', 'b1', 'w2', 'b2')}
    del _L0_ffn_all

    def _L1_attn_setup():
        import jax, jax.numpy as jnp
        import numpy as np
        DIM = 64
        N_SCALES = 4
        PHASES_PER_SCALE = 16
        K_PHASES = N_SCALES * PHASES_PER_SCALE
        B, L = (2, 256)
        key = jax.random.key(seed)
        ks = jax.random.split(key, 16)
        s = 0.02
        d, k = (DIM, K_PHASES)
        return {'x': jax.random.normal(ks[0], (B, L, d), dtype=jnp.float32), 'Wk1': jax.random.normal(ks[1], (d, d), dtype=jnp.float32) * s, 'bk1': jnp.zeros((d,), jnp.float32), 'Wk2': jax.random.normal(ks[2], (d, k), dtype=jnp.float32) * s, 'bk2': jnp.zeros((k,), jnp.float32), 'Wq1': jax.random.normal(ks[3], (d, d), dtype=jnp.float32) * s, 'bq1': jnp.zeros((d,), jnp.float32), 'Wq2': jax.random.normal(ks[4], (d, k), dtype=jnp.float32) * s, 'bq2': jnp.zeros((k,), jnp.float32), 'Wv': jax.random.normal(ks[5], (d, d), dtype=jnp.float32) * s, 'bv': jnp.zeros((d,), jnp.float32), 'ln_w': jnp.ones((d,), jnp.float32), 'ln_b': jnp.zeros((d,), jnp.float32), 'Wo': jax.random.normal(ks[6], (d, d), dtype=jnp.float32) * s, 'bo': jnp.zeros((d,), jnp.float32)}
    _L1_attn_all = _L1_attn_setup()
    _L1_attn_in = {k: v for k, v in _L1_attn_all.items() if k in ('Wk1', 'bk1', 'Wk2', 'bk2', 'Wq1', 'bq1', 'Wq2', 'bq2', 'Wv', 'bv', 'ln_w', 'ln_b', 'Wo', 'bo')}
    del _L1_attn_all

    def _L1_ffn_setup():
        import jax, jax.numpy as jnp
        import numpy as np
        D_MODEL = 64
        EXPERT_DIM = 128
        NUM_EXPERTS = 8
        TOP_K = 2
        SEQ_LEN = 512
        BATCH = 2
        key = jax.random.key(seed)
        ks = jax.random.split(key, 8)
        s = 0.02
        x = jax.random.normal(ks[0], (SEQ_LEN, BATCH, D_MODEL), dtype=jnp.float32)
        Wg = jax.random.normal(ks[1], (D_MODEL, NUM_EXPERTS), dtype=jnp.float32) * s
        bg = jax.random.normal(ks[2], (NUM_EXPERTS,), dtype=jnp.float32) * s
        bias = jnp.zeros((NUM_EXPERTS,), dtype=jnp.float32)
        W1 = jax.random.normal(ks[3], (NUM_EXPERTS, D_MODEL, EXPERT_DIM), dtype=jnp.float32) * s
        b1 = jax.random.normal(ks[4], (NUM_EXPERTS, EXPERT_DIM), dtype=jnp.float32) * s
        W2 = jax.random.normal(ks[5], (NUM_EXPERTS, EXPERT_DIM, D_MODEL), dtype=jnp.float32) * s
        b2 = jax.random.normal(ks[6], (NUM_EXPERTS, D_MODEL), dtype=jnp.float32) * s
        return {'x': x, 'Wg': Wg, 'bg': bg, 'bias': bias, 'W1': W1, 'b1': b1, 'W2': W2, 'b2': b2}
    _L1_ffn_all = _L1_ffn_setup()
    _L1_ffn_in = {k: v for k, v in _L1_ffn_all.items() if k in ('Wg', 'bg', 'bias', 'W1', 'b1', 'W2', 'b2')}
    del _L1_ffn_all
    return {'x': x, 'L0_tok_embed_table': _L0_tok_in['embed_table'], 'L0_tok_conv_w': _L0_tok_in['conv_w'], 'L0_tok_proj_w': _L0_tok_in['proj_w'], 'L0_tok_proj_b': _L0_tok_in['proj_b'], 'L0_attn_W_ih_0': _L0_attn_in['W_ih_0'], 'L0_attn_W_hh_0': _L0_attn_in['W_hh_0'], 'L0_attn_b_ih_0': _L0_attn_in['b_ih_0'], 'L0_attn_b_hh_0': _L0_attn_in['b_hh_0'], 'L0_attn_W_ih_1': _L0_attn_in['W_ih_1'], 'L0_attn_W_hh_1': _L0_attn_in['W_hh_1'], 'L0_attn_b_ih_1': _L0_attn_in['b_ih_1'], 'L0_attn_b_hh_1': _L0_attn_in['b_hh_1'], 'L0_attn_fc_w': _L0_attn_in['fc_w'], 'L0_attn_fc_b': _L0_attn_in['fc_b'], 'L0_ffn_attention_mask': _L0_ffn_in['attention_mask'], 'L0_ffn_wr': _L0_ffn_in['wr'], 'L0_ffn_br': _L0_ffn_in['br'], 'L0_ffn_w1': _L0_ffn_in['w1'], 'L0_ffn_b1': _L0_ffn_in['b1'], 'L0_ffn_w2': _L0_ffn_in['w2'], 'L0_ffn_b2': _L0_ffn_in['b2'], 'L1_attn_Wk1': _L1_attn_in['Wk1'], 'L1_attn_bk1': _L1_attn_in['bk1'], 'L1_attn_Wk2': _L1_attn_in['Wk2'], 'L1_attn_bk2': _L1_attn_in['bk2'], 'L1_attn_Wq1': _L1_attn_in['Wq1'], 'L1_attn_bq1': _L1_attn_in['bq1'], 'L1_attn_Wq2': _L1_attn_in['Wq2'], 'L1_attn_bq2': _L1_attn_in['bq2'], 'L1_attn_Wv': _L1_attn_in['Wv'], 'L1_attn_bv': _L1_attn_in['bv'], 'L1_attn_ln_w': _L1_attn_in['ln_w'], 'L1_attn_ln_b': _L1_attn_in['ln_b'], 'L1_attn_Wo': _L1_attn_in['Wo'], 'L1_attn_bo': _L1_attn_in['bo'], 'L1_ffn_Wg': _L1_ffn_in['Wg'], 'L1_ffn_bg': _L1_ffn_in['bg'], 'L1_ffn_bias': _L1_ffn_in['bias'], 'L1_ffn_W1': _L1_ffn_in['W1'], 'L1_ffn_b1': _L1_ffn_in['b1'], 'L1_ffn_W2': _L1_ffn_in['W2'], 'L1_ffn_b2': _L1_ffn_in['b2']}

def reference(x, L0_tok_embed_table, L0_tok_conv_w, L0_tok_proj_w, L0_tok_proj_b, L0_attn_W_ih_0, L0_attn_W_hh_0, L0_attn_b_ih_0, L0_attn_b_hh_0, L0_attn_W_ih_1, L0_attn_W_hh_1, L0_attn_b_ih_1, L0_attn_b_hh_1, L0_attn_fc_w, L0_attn_fc_b, L0_ffn_attention_mask, L0_ffn_wr, L0_ffn_br, L0_ffn_w1, L0_ffn_b1, L0_ffn_w2, L0_ffn_b2, L1_attn_Wk1, L1_attn_bk1, L1_attn_Wk2, L1_attn_bk2, L1_attn_Wq1, L1_attn_bq1, L1_attn_Wq2, L1_attn_bq2, L1_attn_Wv, L1_attn_bv, L1_attn_ln_w, L1_attn_ln_b, L1_attn_Wo, L1_attn_bo, L1_ffn_Wg, L1_ffn_bg, L1_ffn_bias, L1_ffn_W1, L1_ffn_b1, L1_ffn_W2, L1_ffn_b2):
    import jax
    import jax.numpy as jnp

    def _L0_tok_ref(y, embed_table, conv_w, proj_w, proj_b):
        import jax, jax.numpy as jnp
        import numpy as np
        VOCAB = 256
        EMBED_DIM = 128
        OUT_FEATS = 64
        CTX = 2
        GROUPS = OUT_FEATS // 4
        BLANK_ID = 0
        table = embed_table.at[BLANK_ID].set(0.0)
        embed = table[y]
        x = jnp.transpose(embed, (0, 2, 1))
        x = jnp.pad(x, ((0, 0), (0, 0), (CTX - 1, 0)))
        x = jax.lax.conv_general_dilated(x, conv_w, window_strides=(1,), padding='VALID', feature_group_count=GROUPS, dimension_numbers=('NCH', 'OIH', 'NCH'))
        x = jnp.transpose(x, (0, 2, 1))
        out = jax.nn.relu(x)
        out = jnp.einsum('nud,fd->nuf', out, proj_w) + proj_b
        return out

    def _L0_attn_ref(x, W_ih_0, W_hh_0, b_ih_0, b_hh_0, W_ih_1, W_hh_1, b_ih_1, b_hh_1, fc_w, fc_b):
        import jax, jax.numpy as jnp
        import numpy as np
        B, S, I, H, O = (64, 128, 64, 256, 64)

        def _rnn_layer(inp, W_ih, W_hh, b_ih, b_hh):
            pre = jnp.einsum('bsi,hi->bsh', inp, W_ih) + (b_ih + b_hh)
            h0 = jnp.zeros((inp.shape[0], W_hh.shape[0]), dtype=inp.dtype)

            def step(h, p_t):
                h = jnp.tanh(p_t + h @ W_hh.T)
                return (h, h)
            _, hs = jax.lax.scan(step, h0, jnp.swapaxes(pre, 0, 1))
            return jnp.swapaxes(hs, 0, 1)
        h = _rnn_layer(x, W_ih_0, W_hh_0, b_ih_0, b_hh_0)
        h = _rnn_layer(h, W_ih_1, W_hh_1, b_ih_1, b_hh_1)
        return h @ fc_w.T + fc_b

    def _L0_ffn_ref(x, attention_mask, wr, br, w1, b1, w2, b2):
        import jax, jax.numpy as jnp
        import numpy as np
        B, S, D = (8, 1024, 64)
        H = 4 * D
        CAPACITY = 0.5
        b, s, d = x.shape
        weights = (jnp.einsum('bsd,do->bso', x, wr) + br)[..., 0]
        k = max(1, int(CAPACITY * s))
        kk = k - 1 if k > 1 else 1
        _, idx = jax.lax.top_k(weights, k)
        sel_idx = idx[:, :kk]
        sel = jnp.take_along_axis(x, sel_idx[:, :, None], axis=1)
        h = jax.nn.gelu(jnp.einsum('bkd,dh->bkh', sel, w1) + b1)
        y = jnp.einsum('bkh,hd->bkd', h, w2) + b2
        w_sel = jnp.take_along_axis(weights, sel_idx, axis=1)
        y = y * w_sel[..., None]
        batch_idx = jnp.arange(b)[:, None]
        processed = jnp.zeros_like(x).at[batch_idx, sel_idx].set(y)
        return processed + x

    def _L1_attn_ref(x, Wk1, bk1, Wk2, bk2, Wq1, bq1, Wq2, bq2, Wv, bv, ln_w, ln_b, Wo, bo):
        import jax, jax.numpy as jnp
        import numpy as np
        DIM = 64
        N_SCALES = 4
        PHASES_PER_SCALE = 16
        K_PHASES = N_SCALES * PHASES_PER_SCALE
        B, L = (2, 256)
        Bb, Ll, D = x.shape
        K = K_PHASES
        freq = jnp.repeat(2.0 ** jnp.arange(N_SCALES, dtype=jnp.float32), PHASES_PER_SCALE)

        def encode(W1, b1, W2, b2):
            h = jax.nn.gelu(x @ W1 + b1, approximate=False)
            return jnp.tanh(h @ W2 + b2)
        key_phase = encode(Wk1, bk1, Wk2, bk2) * freq * jnp.pi
        query_phase = encode(Wq1, bq1, Wq2, bq2) * freq * jnp.pi
        key_phasor = jnp.cos(key_phase) + 1j * jnp.sin(key_phase)
        query_conj = jnp.cos(query_phase) - 1j * jnp.sin(query_phase)
        V = (x @ Wv + bv).astype(jnp.complex64)
        bound = key_phasor[..., None] * V[:, :, None, :]
        memory = jnp.cumsum(bound, axis=1)
        retrieved = jnp.real(jnp.sum(memory * query_conj[..., None], axis=2))
        positions = jnp.arange(1, Ll + 1, dtype=jnp.float32)
        retrieved = retrieved / jnp.sqrt(positions * K)[None, :, None]
        mu = jnp.mean(retrieved, axis=-1, keepdims=True)
        var = jnp.var(retrieved, axis=-1, keepdims=True)
        normed = (retrieved - mu) / jnp.sqrt(var + 1e-05) * ln_w + ln_b
        return x + normed @ Wo + bo

    def _L1_ffn_ref(x, Wg, bg, bias, W1, b1, W2, b2):
        import jax, jax.numpy as jnp
        import numpy as np
        D_MODEL = 64
        EXPERT_DIM = 128
        NUM_EXPERTS = 8
        TOP_K = 2
        SEQ_LEN = 512
        BATCH = 2
        x_flat = x.reshape(-1, D_MODEL)
        gate_logits = x_flat @ Wg + bg + bias
        topk_vals, topk_idx = jax.lax.top_k(gate_logits, TOP_K)
        topk_w = jax.nn.softmax(topk_vals, axis=-1)
        combine = (jax.nn.one_hot(topk_idx, NUM_EXPERTS, dtype=x.dtype) * topk_w[..., None]).sum(axis=1)
        h = jax.nn.relu(jnp.einsum('td,edh->teh', x_flat, W1) + b1)
        y = jnp.einsum('teh,ehd->ted', h, W2) + b2
        out = jnp.einsum('ted,te->td', y, combine)
        return out.reshape(x.shape)
    h = _L0_tok_ref(x, L0_tok_embed_table, L0_tok_conv_w, L0_tok_proj_w, L0_tok_proj_b)
    h = h + _L0_attn_ref(_layernorm(h, axis=-1), L0_attn_W_ih_0, L0_attn_W_hh_0, L0_attn_b_ih_0, L0_attn_b_hh_0, L0_attn_W_ih_1, L0_attn_W_hh_1, L0_attn_b_ih_1, L0_attn_b_hh_1, L0_attn_fc_w, L0_attn_fc_b)
    h = h + _L0_ffn_ref(_layernorm(h, axis=-1), L0_ffn_attention_mask, L0_ffn_wr, L0_ffn_br, L0_ffn_w1, L0_ffn_b1, L0_ffn_w2, L0_ffn_b2)
    h = h + _L1_attn_ref(_layernorm(h, axis=-1), L1_attn_Wk1, L1_attn_bk1, L1_attn_Wk2, L1_attn_bk2, L1_attn_Wq1, L1_attn_bq1, L1_attn_Wq2, L1_attn_bq2, L1_attn_Wv, L1_attn_bv, L1_attn_ln_w, L1_attn_ln_b, L1_attn_Wo, L1_attn_bo)
    h = h + _L1_ffn_ref(_layernorm(h, axis=-1), L1_ffn_Wg, L1_ffn_bg, L1_ffn_bias, L1_ffn_W1, L1_ffn_b1, L1_ffn_W2, L1_ffn_b2)
    return h

_drawn_inputs = setup_inputs


def setup_inputs(seed=0):
    import zlib

    import numpy as np

    out = dict(_drawn_inputs(seed))
    spreads = {'L0_ffn_b1': (0.0, 0.8),
     'L0_ffn_b2': (0.0, 0.406),
     'L1_attn_bk1': (0.0, 0.8),
     'L1_attn_bk2': (0.0, 0.8),
     'L1_attn_bq1': (0.0, 0.8),
     'L1_attn_bq2': (0.0, 0.8),
     'L1_attn_bv': (0.0, 0.1),
     'L1_attn_ln_w': (1.0, 0.6),
     'L1_attn_ln_b': (0.0, 0.8),
     'L1_attn_bo': (0.0, 0.1),
     'L1_ffn_bias': (0.0, 0.8)}
    factors = {'L0_ffn_wr': 4.362,
     'L0_ffn_w1': 8.0,
     'L0_ffn_w2': 8.0,
     'L1_attn_Wk1': 8.0,
     'L1_attn_Wk2': 8.0,
     'L1_attn_Wq1': 8.0,
     'L1_attn_Wq2': 8.0,
     'L1_ffn_Wg': 6.001,
     'L1_ffn_bg': 8.0,
     'L1_ffn_W1': 8.0,
     'L1_ffn_b1': 8.0,
     'L1_ffn_W2': 8.0,
     'L1_ffn_b2': 7.992}
    for name, (base, spread) in spreads.items():
        noise = np.random.default_rng([zlib.crc32(name.encode()), seed]).standard_normal(out[name].shape)
        drawn = base * np.exp(spread * noise) if base else spread * noise
        out[name] = jnp.asarray(drawn.astype(out[name].dtype))
    for name, factor in factors.items():
        out[name] = (out[name] * factor).astype(out[name].dtype)
    return out
```

```python
from contextlib import ExitStack

import numpy as np

import concourse.bass as bass
from concourse import mybir

ALU = mybir.AluOpType
ACT = mybir.ActivationFunctionType
F32 = mybir.dt.float32
F16 = mybir.dt.float16
BF16 = mybir.dt.bfloat16
I32 = mybir.dt.int32
AX = mybir.AxisListType
RMAX = bass.bass_isa.ReduceOp.max

P = 128
KEEP = 511
B, T = 8, 1024
D = 64
H = 256
KH = H // P
TT = T // P
NT = B * TT
VOC = 256
NE, HE = 8, 128
U = 32
LAG = 14
OFF = U + LAG
BODY = 2 * U
EPS = 1e-5
TWO_PI = 2.0 * np.pi
MAGIC = 1.5 * 2.0 ** 23

W_IH0, W_FF1, W_KQ1, W_V, W_G, W_E1, W_END = 0, 256, 512, 640, 704, 712, 1736


NORMS = 5


class Chain:

    def __init__(self, eng, sem):
        self.eng, self.sem, self.base, self.n, self.i, self.per = eng, sem, 0, 0, None, 0

    def __call__(self, ins):
        ins.then_inc(self.sem, 1)
        self.n += 1
        at = self.base + self.n
        self.eng.wait_ge(self.sem, at if self.i is None else self.i * self.per + at)

    def loop(self, i, per):
        self.base, self.n, self.i, self.per = self.base + self.n, 0, i, per

    def end(self, count):
        assert self.n == self.per, (self.n, self.per)
        self.base, self.n, self.i = self.base + self.per * count, 0, None


def build(nc, a, out, stop=99):
    with ExitStack() as ctx:
        def sb(name, shape, dt=F32):
            return ctx.enter_context(nc.sbuf_tensor(name, shape, dt))

        def sem(name):
            return ctx.enter_context(nc.semaphore(name))

        bank = [ctx.enter_context(nc.psum_tensor(f"bank{i}", [P, 512], F32)) for i in range(8)]
        sum0, sum1 = bank[0:2], bank[2:4]

        res = sb("res", [P, NT, D])
        yw = sb("yw", [P, NT, D])
        wr = sb("wr", [P, NT])
        pick = sb("pick", [P, NT])
        xt = sb("xt", [P, B * T], F16)
        xr = sb("xr", [P, T, B], F16)
        all_hi = sb("all_hi", [P, KH, B, T], F16)
        all_lo = sb("all_lo", [P, KH, B, T], F16)
        eye = sb("eye", [P, P])
        eye16 = sb("eye16", [P, P], F16)
        wx = [sb(f"wx{i}", [P, W_END], BF16) for i in range(3)]
        whh_hi = [sb(f"whh{l}_hi", [P, KH, H], F16) for l in range(2)]
        whh_lo = [sb(f"whh{l}_lo", [P, KH, H], F16) for l in range(2)]
        wih1_hi = sb("wih1_hi", [P, KH, H], F16)
        wih1_lo = sb("wih1_lo", [P, KH, H], F16)
        wfc_hi = sb("wfc_hi", [P, KH, D], F16)
        wfc_lo = sb("wfc_lo", [P, KH, D], F16)
        bias = sb("bias", [P, 2, H], BF16)
        ones = sb("ones", [P, U * B], BF16)
        scl = sb("scl", [P, 3])
        inv = sb("inv", [P, 3])
        stat = sb("stat", [P, 8, 8])
        fcb = sb("fcb", [P, D])
        cur = sb("cur", [P, TT, D])
        nrm = sb("nrm", [P, TT, D])
        xc = sb("xc", [P, TT, D])
        sq = sb("sq", [P, TT, D])
        tmp8 = sb("tmp8", [P, TT, D])
        xs = sb("xs", [P, TT, 2, D], F16)
        nhalf = sb("nhalf", [P, TT])

        s_w = sem("weights_loaded")
        s_ids = [sem(f"ids_loaded{i}") for i in range(4)]
        s_out = sem("out_written")
        dve_chain, act_chain, pool_chain = sem("dve_order"), sem("act_order"), sem("pool_order")

        s_mx = sem("largest_weights")
        s_mxa = sem("largest_weights_all")
        s_tab = sem("table_summed")
        s_tabw = sem("table_split")
        s_prep = sem("weights_ready")
        s_pinit = sem("pool_constants")
        s_oh = sem("onehot_ready")
        s_conv = sem("conv_summed")
        s_relu = sem("conv_relu")
        s_proj = sem("proj_summed")
        s_projr = sem("proj_read")
        s_nrm = sem("normalised")
        s_xc, s_sq, s_var, s_rstd, s_xs, s_tr, s_xt = (
            sem(n) for n in ("centred", "squared", "variance", "rstd", "norm_split", "norm_turned", "norm_copied"))
        s_sum = [sem("sum0_ready"), sem("sum1_ready")]
        s_h = [sem("state0_ready"), sem("state1_ready")]
        s_lo = [sem("state0_low"), sem("state1_low")]
        s_keep = sem("state1_kept")
        s_fc = sem("fc_summed")
        s_fcr = sem("fc_read")
        s_done = sem("all_done")
        s_fcb = sem("pool_tail")
        s_ff, s_g, s_y, s_yc, s_yt, s_ytr = (
            sem(n) for n in ("ff_hidden", "ff_gelu", "ff_summed", "ff_copied", "ff_turned", "ff_kept"))
        s_wr, s_wt, s_wtc, s_wdram, s_wall, s_enough, s_digit = (
            sem(n) for n in ("router_ready", "router_turned", "router_copied", "router_in_dram", "router_spread",
                             "enough_above", "digit_counted"))
        s_thr, s_thr_all, s_above, s_counted = (
            sem(n) for n in ("threshold", "threshold_spread", "above_ready", "above_counted"))
        s_kq, s_kqg, s_ph, s_th, s_thr_r, s_v, s_vr = (
            sem(n) for n in ("kq_hidden", "kq_gelu", "kq_phase", "kq_tanh", "phase_kept", "values_summed", "values_kept"))
        s_phi, s_s, s_sm, s_k, s_kt, s_st, s_stc, s_rt = (
            sem(n) for n in ("phasors", "scores", "scores_masked", "keys_turned", "keys_copied", "memory_summed",
                             "memory_copied", "attention_kept"))
        s_nt, s_ntc, s_wo, s_wor = (sem(n) for n in ("att_turned", "att_scaled", "att_projected", "att_added"))
        s_gt, s_lm, s_ex, s_cp, s_ct, s_ctc = (
            sem(n) for n in ("gates_summed", "gates_shifted", "gates_exp", "weights_split", "weights_turned",
                             "weights_copied"))
        s_hid, s_r, s_c, s_gp, s_moe, s_moec, s_moet, s_fin = (
            sem(n) for n in ("expert_hidden", "expert_relu", "expert_weight", "expert_weighted", "experts_summed",
                             "experts_copied", "experts_turned", "sequence_done"))

        names = ("wr_row", "bo", "bv", "ff_b2", "gb")
        row = {n: sb("row_" + n, [P, a[n].shape[0]]) for n in names}
        col = sb("col", [P, 16])
        ebias = sb("ebias", [P, NE])
        ffw2 = sb("ffw2", [P, KH, D])
        wkq2 = sb("wkq2", [P, P])
        wobd = sb("wobd", [P, P])
        ew2 = sb("ew2", [P, NE, D])
        eb2 = sb("eb2", [P, D])
        eb2p = sb("eb2p", [P, 3, D], BF16)
        self32 = sb("self32", [P, NE, P])
        sel16 = sb("sel16", [P, NE, P], BF16)
        eye_b = sb("eye_b", [P, P], BF16)
        tri = sb("tri", [P, P])
        trix = sb("trix", [P, P])
        ones32 = sb("ones32", [P, P])
        group = sb("group", [P, P])
        first8 = sb("first8", [P, B])
        digit = sb("digit", [P, 8], I32)
        posr = sb("posr", [P, TT])
        order = sb("order", [P, NE, NE])
        router_dram = nc.dram_tensor("router_dram", (B, T), F32, kind="Internal").ap()

        ph = ExitStack()

        def tmp(name, shape, dt=F32):
            return ph.enter_context(nc.sbuf_tensor(name, shape, dt))

        lo_space = all_lo[:, :, :, :].rearrange("p k b t -> p (k b t)").bitcast(F32)
        hi_space = all_hi[:, :, :, :].rearrange("p k b t -> p (k b t)")
        big = lo_space[:, 0:W_END]
        rest = lo_space[:, W_END:2 * W_END]
        wrec = lo_space[:, 2 * W_END:2 * W_END + 3 * KH * H].rearrange("p (i k h) -> p i k h", i=3, k=KH)
        wfc = tmp("wfc", [P, KH, D])
        brec = tmp("brec", [P, 4, H])
        bsum = tmp("bsum", [P, 2, H])
        bpart = tmp("bpart", [P, 2, H], BF16)
        embt = tmp("embt", [P, VOC])
        wconv = tmp("wconv", [P, 2, P])
        tab = [tmp(f"tab{i}", [P, 2, 2, P], BF16) for i in range(3)]
        wproj = tmp("wproj", [P, D])
        bproj = tmp("bproj", [P, D])
        vid = tmp("vid", [P, 2])
        ids = hi_space.bitcast(I32).rearrange("p (b t) -> p b t", b=B)
        onehot = tmp("onehot", [P, 2, T + 2], BF16)
        relu = tmp("relu", [P, 2, 512])
        h_hi = [tmp(f"h{l}_hi", [P, 2, KH, U, B], F16) for l in range(2)]
        h_lo = [tmp(f"h{l}_lo", [P, 2, KH, U, B], F16) for l in range(2)]
        h_f = [tmp(f"h{l}_f", [P, 2, KH, B]) for l in range(2)]

        loads = [
            (big[:, :], a["wx"]), (wrec[:, :, :, :], a["wrec"]), (wfc[:, :, :], a["wfc"]),
            (brec[:, :, :].rearrange("p a h -> p (a h)"), a["brec"].partition_broadcast(P)),
            (embt[:, :], a["embt"]), (wconv[:, :, :], a["wconv"]), (wproj[:, :], a["wproj"]),
            (bproj[:, :], a["proj_b"].partition_broadcast(P)), (fcb[:, :], a["fc_b"].partition_broadcast(P)),
            *((row[n][:, :], a[n].partition_broadcast(P)) for n in names),
            (col[:, :], a["col"]), (ebias[:, :], a["ebias"]), (ffw2[:, :, :], a["ffw2"]), (wkq2[:, :], a["wkq2"]),
            (wobd[:, :], a["wobd"]), (ew2[:, :, :], a["ew2"]), (eb2[:, :], a["eb2"]), (self32[:, :, :], a["self32"]),
            (tri[:, :], a["tri"]), (trix[:, :], a["trix"]), (group[:, :], a["group"]), (first8[:, :], a["first8"]),
            (digit[:, :], a["digit"]), (posr[:, :], a["posr"]),
            (order[:, :, :], a["order"]),
            (vid[:, :], a["vid"]), (eye[:, :], a["eye"]), (eye16[:, :], a["eye16"]),
        ]

        def spread(x):
            return x.unsqueeze(2).to_broadcast([P, TT, D])

        def rows(x):
            return x.unsqueeze(1).to_broadcast([P, TT, D])

        def tokens(x):
            return x.rearrange("p (t d) -> p t d", t=TT)

        def norm_vector(dve, link, k, src=cur):
            link(dve.reduce_sum(stat[:, 0, :], src[:, :, :], AX.X))
            link(dve.tensor_scalar(stat[:, 1, :], stat[:, 0, :], 1.0 / D, None, ALU.mult))
            dve.tensor_tensor(xc[:, :, :], src[:, :, :], spread(stat[:, 1, :]), ALU.subtract).then_inc(s_xc, 1)
            dve.wait_ge(s_sq, k + 1)
            link(dve.reduce_sum(stat[:, 2, :], sq[:, :, :], AX.X))
            dve.tensor_scalar(stat[:, 3, :], stat[:, 2, :], 1.0 / D, EPS, ALU.mult, ALU.add).then_inc(s_var, 1)
            dve.wait_ge(s_rstd, k + 1)
            dve.tensor_tensor(nrm[:, :, :], xc[:, :, :], spread(stat[:, 4, :]), ALU.mult).then_inc(s_nrm, 1)
            dve.wait_ge(s_nrm, k + 1)

        def norm_split(dve, link, k):
            dve.wait_ge(s_tr, k)
            link(dve.tensor_copy(xs[:, :, 0, :], nrm[:, :, :]))
            dve.tensor_tensor(xs[:, :, 1, :], nrm[:, :, :], xs[:, :, 0, :], ALU.subtract).then_inc(s_xs, 1)

        def norm_square(act, k):
            act.wait_ge(s_xc, k + 1)
            act.activation(sq[:, :, :], xc[:, :, :], ACT.Square).then_inc(s_sq, 1)

        def norm_rstd(pool, k):
            pool.wait_ge(s_var, k + 1)
            pool.tensor_tensor(stat[:, 4, :], stat[:, 3, :], nhalf[:, :], ALU.pow).then_inc(s_rstd, 1)

        def norm_turn(pe, dst, k):
            pe.wait_ge(s_xs, k + 1)
            pe.wait_ge(s_xt, k)
            for t in range(TT):
                mm = pe.transpose(dst.bitcast(F16)[:, t * P:(t + 1) * P],
                                  xs[:, t, :, :].rearrange("p a d -> p (a d)"), eye16[:, :])
            mm.then_inc(s_tr, 1)

        def norm_copy(act, dst, src, k):
            act.wait_ge(s_tr, k + 1)
            act.activation(dst, src.bitcast(F16)[:, 0:T], ACT.Copy).then_inc(s_xt, 1)

        def rec_tensor(pe, g, j, l0, l1):
            def step(layer, s):
                q, u = (s // U) % 2, s % U
                pq, pu = ((s - 1) // U) % 2, (s - 1) % U
                at = j * BODY + s
                pe.wait_ge(s_h[layer], at)
                sums = (sum0, sum1)[layer][q][:, :].rearrange("p (m s b) -> p m s b", m=KH, s=U)
                for w in (whh_hi, whh_lo):
                    for m in range(KH):
                        for k in range(KH):
                            pe.matmul(sums[:, m, u, :], w[layer][:, k, m * P:(m + 1) * P],
                                      h_hi[layer][:, pq, k, pu, :], start=False, stop=False,
                                      skip_group_check=True)
                pe.wait_ge(s_lo[layer], at)
                for m in range(KH):
                    for k in range(KH):
                        mm = pe.matmul(sums[:, m, u, :], whh_hi[layer][:, k, m * P:(m + 1) * P],
                                       h_lo[layer][:, pq, k, pu, :], start=False, stop=False,
                                       skip_group_check=True)
                mm.then_inc(s_sum[layer], 1)

            if l0:
                step(0, g)
            u = g % U
            if u > LAG and g // U + 1 < T // U:
                before0(pe, g // U + 1, j, u - LAG - 1)
            if U <= g < T + U and u < LAG:
                before1(pe, g // U - 1, u)
            if l1:
                step(1, g - OFF)

        def before0(pe, n, j, i):
            sums = sum0[n % 2][:, :].rearrange("p (m c) -> p m c", m=KH)
            if i >= 8:
                return
            m, part = i // 4, i % 4
            if part == 0:
                pe.matmul(sums[:, m, :], bias[:, 0, m * P:(m + 1) * P], ones[:, :],
                          start=(m == 0), stop=False, skip_group_check=True)
            else:
                x = xr[:, :, :].rearrange("p t b -> p (t b)")
                pe.matmul(sums[:, m, :], wx[part - 1][:, W_IH0 + m * P:W_IH0 + (m + 1) * P],
                          x[:, bass.ds(j * (BODY * B) + n * U * B, U * B)],
                          start=False, stop=False, skip_group_check=True)

        def before1(pe, n, i):
            sums = sum1[n % 2][:, :].rearrange("p (m c) -> p m c", m=KH)
            m, part = i // 7, i % 7
            if part == 0:
                pe.matmul(sums[:, m, :], bias[:, 1, m * P:(m + 1) * P], ones[:, :],
                          start=(m == 0), stop=False, skip_group_check=True)
            else:
                w, h = ((wih1_hi, h_hi), (wih1_lo, h_hi), (wih1_hi, h_lo))[(part - 1) // 2]
                k = (part - 1) % 2
                pe.matmul(sums[:, m, :], w[:, k, m * P:(m + 1) * P],
                          h[0][:, n % 2, k, :, :].rearrange("p s b -> p (s b)"),
                          start=False, stop=False, skip_group_check=True)

        def rec_scalar(act, g, j, l0, l1, scale):
            for layer, on, s in ((0, l0, g), (1, l1, g - OFF)):
                if not on:
                    continue
                q, u = (s // U) % 2, s % U
                if layer == 1 and u == 0:
                    act.wait_ge(s_keep, j * 2 + s // U)
                sums = (sum0, sum1)[layer][q][:, :].rearrange("p (m s b) -> p m s b", m=KH, s=U)
                act.wait_ge(s_sum[layer], j * BODY + s + 1)
                act.activation(h_hi[layer][:, q, :, u, :], sums[:, :, u, :], ACT.Tanh, scale=scale[layer])
                act.activation(h_f[layer][:, s % 2, :, :], sums[:, :, u, :], ACT.Tanh,
                               scale=scale[layer]).then_inc(s_h[layer], 1)

        def rec_vector(dve, g, j, l0, l1):
            for layer, on, s in ((0, l0, g), (1, l1, g - OFF)):
                if not on:
                    continue
                q, u = (s // U) % 2, s % U
                dve.wait_ge(s_h[layer], j * BODY + s + 1)
                dve.tensor_tensor(h_lo[layer][:, q, :, u, :], h_f[layer][:, s % 2, :, :],
                                  h_hi[layer][:, q, :, u, :], ALU.subtract).then_inc(s_lo[layer], 1)

        def recurrence(eng, slot):
            count = (T - OFF) // BODY
            for g in range(OFF):
                slot(eng, g, 0, True, False)
            with eng.Fori(0, count) as j:
                for g in range(OFF, OFF + BODY):
                    slot(eng, g, j, True, True)
            for g in range(OFF + BODY * count, T + OFF):
                slot(eng, g, 0, g < T, True)

        ph.close()
        ph = ctx.enter_context(ExitStack())
        rph = hi_space.bitcast(F32)
        vv = xr[:, :, :].rearrange("p t b -> p (t b)").bitcast(F32).rearrange("p (n d) -> p n d", d=D)
        gel = tmp("gel", [P, 2, KH, 512])
        yt = tmp("yt", [P, 512])
        th = tmp("th", [P, 2, 512])
        turns = tmp("turns", [P, 512])
        whole = tmp("whole", [P, 512])
        lo2 = lo_space
        wall = lo2[:, 0:T]
        junk = lo2[:, T:T + 512].bitcast(BF16)
        wt = lo2[:, 1536:1536 + P]
        above, equal, before, offs = (lo2[:, 1700 + 64 * i:1764 + 64 * i] for i in range(4))
        key, cand, flip, fbits, digi = (lo2[:, 2000 + i:2001 + i].bitcast(I32) for i in range(5))
        cnt, enough = (lo2[:, 2010 + i:2011 + i] for i in range(2))
        thr8, sum8 = (lo2[:, 2020 + 8 * i:2028 + 8 * i] for i in range(2))
        rabs = lo2[:, 2048:3072]
        phk, phq = (lo2[:, 3072 + 2048 * i:3072 + 2048 * (i + 1)].rearrange("p (q t) -> p q t", q=2) for i in range(2))
        sm = lo2[:, 7168:7424].rearrange("p (q t) -> p q t", q=2)
        kt = lo2[:, 7424:7680].rearrange("p (q t) -> p q t", q=2)
        stc = lo2[:, 7680:7744]
        ntb = turns
        lg, gex = tmp("lg", [P, TT, NE]), tmp("gex", [P, TT, NE])
        gdiff = tmp("gdiff", [P, TT, NE, NE])
        grank, gsel, gc, gleft = (tmp(n, [P, TT, NE]) for n in ("grank", "gsel", "gc", "gleft"))
        cp = tmp("cp", [P, TT, P], BF16)
        ct = tmp("ct", [P, T], BF16)
        gr = gel
        gp = tmp("gp", [P, 2, 2, 512])

        def skewed(eng, front, back, link=None, links=0, last=lambda b: None):
            front(0)
            last(0)
            with eng.Fori(0, B - 1) as b:
                if link:
                    link.loop(b, links)
                front(b + 1)
                back(b)
                last(b + 1)
                if link:
                    link.end(B - 1)
            back(B - 1)

        (FF_B1, KQ_B1, KQ_B2, LN_W, LN_B, TURN, WR_B) = (0, 2, 3, 4, 5, 6, 7)
        column = lambda i: col[:, i:i + 1]
        span = lambda b: bass.ds(b * TT, TT)

        block = ctx.enter_context(nc.Block())

        @block.sync
        def _(sp):
            for i in range(4):
                sp.dma_start(ids[:, 2 * i:2 * i + 2, :],
                             a["x"][2 * i:2 * i + 2, :].partition_broadcast(P)).then_inc(s_ids[i], 16)
                if i == 0:
                    for dst, src in loads:
                        sp.dma_start(dst, src).then_inc(s_w, 16)
            if stop <= 1:
                sp.wait_ge(s_fcr, B)
                sp.wait_ge(s_ytr, B)
                sp.dma_start(out.rearrange("b (t p) d -> p (b t) d", p=P), res[:, :, :]).then_inc(s_out, 16)
                sp.wait_ge(s_out, 16)
                return
            sp.wait_ge(s_wtc, 1)
            sp.dma_start(router_dram.rearrange("b (t p) -> (b t) p", p=P), wt[0:NT, :]).then_inc(s_wdram, 16)
            sp.wait_ge(s_wdram, 16)
            for b in range(B):
                sp.dma_start(wall[b * 16:b * 16 + 16, :],
                             router_dram[b:b + 1, :].partition_broadcast(16)).then_inc(s_wall, 16)
            if stop <= 4:
                sp.wait_ge(s_done, 1)
                sp.dma_start(out.rearrange("b (t p) d -> p (b t) d", p=P), res[:, :, :]).then_inc(s_out, 16)
                sp.wait_ge(s_out, 16)
                return
            for b in range(B):
                sp.wait_ge(s_fin, b + 1)
                sp.dma_start(out[b].rearrange("(t p) d -> p t d", p=P),
                             res[:, b * TT:(b + 1) * TT, :]).then_inc(s_out, 16)
            sp.wait_ge(s_out, 16 * B)

        @block.gpsimd
        def _(pool):
            pool.memset(nhalf[:, :], -0.5).then_inc(s_pinit, 1)
            for l in range(2):
                pool.memset(h_hi[l][:, 1, :, U - 1, :], 0.0).then_inc(s_pinit, 1)
                pool.memset(h_lo[l][:, 1, :, U - 1, :], 0.0).then_inc(s_pinit, 1)
            pool.memset(ones[:, :], 1.0).then_inc(s_pinit, 1)
            pool.memset(bias[:, :, :], 0.0).then_inc(s_pinit, 1)
            pool.memset(onehot[:, :, 0:1], 0.0).then_inc(s_pinit, 1)
            pool.memset(stat[:, 5, 7:8], 0.0).then_inc(s_keep, 1)
            pool.memset(ones32[:, :], 1.0).then_inc(s_pinit, 1)
            pool.wait_ge(s_pinit, 9)
            pool.wait_ge(s_mx, 1)
            pool.partition_all_reduce(stat[:, 6, 0:3], stat[:, 5, 0:3], P, RMAX).then_inc(s_mxa, 1)
            with pool.Fori(0, B) as b:
                norm_rstd(pool, b)
            with pool.Fori(0, T // BODY) as j:
                for q in range(2):
                    pool.wait_ge(s_h[1], j * BODY + (q + 1) * U)
                    pool.wait_ge(s_lo[1], j * BODY + (q + 1) * U)
                    for k in range(KH):
                        for dst, src in ((all_hi, h_hi), (all_lo, h_lo)):
                            ins = pool.tensor_copy(dst[:, k, :, bass.ds(j * BODY + q * U, U)],
                                                   src[1][:, q, k, :, :].rearrange("p s b -> p b s"))
                    ins.then_inc(s_keep, 1)

            pool.wait_ge(s_keep, T // U + 1)
            pool.wait_ge(s_lo[1], T)
            pool.memset(cp[:, :, :], 0.0).then_inc(s_fcb, 1)
            if stop <= 1:
                for b in range(B):
                    norm_rstd(pool, B + b)
                return
            with pool.Fori(0, (NORMS - 1) * B) as n:
                norm_rstd(pool, B + n)

        @block.scalar
        def _(act):
            act.wait_ge(s_prep, 1)
            rescale = []
            for l in range(2):
                r = act.alloc_register(f"rescale{l}")
                act.reg_load(r, inv[0:1, l:l + 1].bitcast(I32))
                rescale.append(r)
            with act.Fori(0, B) as b:
                for half in range(2):
                    act.wait_ge(s_conv, b * 2 + half + 1)
                    act.wait_ge(s_proj, b)
                    act.activation(relu[:, half, :], bank[half][:, :], ACT.Relu).then_inc(s_relu, 1)
                norm_square(act, b)
                norm_copy(act, xr[:, :, bass.ds(b, 1)].rearrange("p t b -> p (t b)"), bank[3], b)
            recurrence(act, lambda e, g, j, l0, l1: rec_scalar(e, g, j, l0, l1, rescale))


            def front(b):
                norm_square(act, B + b)

            def last(b):
                norm_copy(act, xt[:, bass.ds(b * T, T)], bank[1], B + b)

            def back(b):
                act.wait_ge(s_y, b)
                for half in range(2):
                    for m in range(KH):
                        act.wait_ge(s_ff, b * 4 + half * 2 + m + 1)
                        act.activation(gel[:, half, m, :], bank[2 + m][:, :], ACT.Gelu_apprx_tanh,
                                       bias=column(FF_B1 + m)).then_inc(s_g, 1)
                act.wait_ge(s_y, b + 1)
                act.wait_ge(s_yt, b)
                act.activation(yt[:, :], bank[4][:, :], ACT.Copy).then_inc(s_yc, 1)

            act.wait_ge(s_h[1], T)
            skewed(act, front, back, last=last)
            if stop <= 1:
                return

            act.wait_ge(s_wt, 1)
            act.activation(wt[0:NT, :], bank[0][0:NT, 0:P], ACT.Copy).then_inc(s_wtc, 1)

            def front(b):
                norm_square(act, 2 * B + b)

            def last(b):
                norm_copy(act, xt[:, bass.ds(b * T, T)], bank[1], 2 * B + b)

            def back(b):
                for half in range(2):
                    act.wait_ge(s_kq, b * 2 + half + 1)
                    act.wait_ge(s_ph, b * 2 + half)
                    act.activation(gel[:, half, 0, :], bank[2][:, :], ACT.Gelu, bias=column(KQ_B1)).then_inc(s_kqg, 1)
                    act.wait_ge(s_ph, b * 2 + half + 1)
                    act.wait_ge(s_thr_r, b * 2)
                    act.activation(th[:, half, :], bank[4][:, :], ACT.Tanh, bias=column(KQ_B2)).then_inc(s_th, 1)

            skewed(act, front, back, last=last)

            act.wait_ge(s_thr_r, 2 * B)
            with act.Fori(0, B // 2) as j:
                for q in range(2):
                    b = j * 2 + q
                    own = rph[:, bass.ds(b * T, T)]
                    act.wait_ge(s_rt, j * 2)
                    act.wait_ge(s_phi, b)
                    act.activation(rabs[:, :], own, ACT.Abs).then_inc(act_chain, 1)
                    act.wait_ge(act_chain, b + 1)
                    act.activation(phk[0:D, q, :], rabs[0:D, :], ACT.Sin, bias=col[0:D, TURN:TURN + 1], scale=-TWO_PI)
                    act.activation(phk[D:P, q, :], rph[0:D, bass.ds(b * T, T)], ACT.Sin, scale=TWO_PI)
                    act.activation(phq[0:D, q, :], rabs[D:P, :], ACT.Sin, bias=col[D:P, TURN:TURN + 1], scale=-TWO_PI)
                    act.activation(phq[D:P, q, :], rph[D:P, bass.ds(b * T, T)], ACT.Sin, scale=TWO_PI).then_inc(s_phi, 1)

            def front(b):
                norm_square(act, 3 * B + b * 2)
                act.wait_ge(s_nt, b + 1)
                act.wait_ge(s_wo, b)
                act.activation(ntb[:, :], bank[0][:, :], ACT.Identity, bias=column(LN_B),
                               scale=column(LN_W)).then_inc(s_ntc, 1)
                norm_square(act, 3 * B + b * 2 + 1)
                norm_copy(act, xt[:, bass.ds(b * T, T)], bank[3], 3 * B + b)
                act.wait_ge(s_lm, b + 1)
                act.activation(gex[:, :, :], gc[:, :, :], ACT.Exp).then_inc(s_ex, 1)

            def back(b):
                act.wait_ge(s_ct, b + 1)
                act.wait_ge(s_moe, b)
                act.activation(ct[:, :], bank[3].bitcast(BF16)[:, 0:T], ACT.Copy).then_inc(s_ctc, 1)
                for e in range(NE):
                    for half in range(2):
                        n = b * 16 + e * 2 + half
                        act.wait_ge(s_hid, n + 1)
                        act.wait_ge(s_gp, b * 16 + max(0, e * 2 + half - 3))
                        act.activation(gr[:, e % 2, half, :], bank[4 + half][:, :], ACT.Relu,
                                       bias=ebias[:, e:e + 1]).then_inc(s_r, 1)
                act.wait_ge(s_moe, b + 1)
                act.wait_ge(s_moet, b)
                act.activation(yt[:, :], bank[2][:, :], ACT.Copy).then_inc(s_moec, 1)

            with act.Fori(0, B) as b:
                front(b)
                back(b)

        @block.tensor
        def _(pe):
            pe.wait_ge(s_w, 16 * len(loads))
            pe.wait_ge(s_tabw, 1)
            for v in range(2):
                for tap in range(2):
                    mm = pe.matmul(bank[0][:, (v * 2 + tap) * P:(v * 2 + tap + 1) * P],
                                   embt[:, v * P:(v + 1) * P], wconv[:, tap, :], start=True, stop=True,
                                   skip_group_check=True)
            mm.then_inc(s_tab, 1)
            pe.wait_ge(s_tabw, 2)
            with pe.Fori(0, B) as b:
                pe.wait_ge(s_oh, b + 1)
                for half in range(2):
                    pe.wait_ge(s_relu, b * 2 + half)
                    n = 0
                    for v in range(2):
                        for tap in range(2):
                            for part in range(3):
                                n += 1
                                mm = pe.matmul(bank[half][:, :], tab[part][:, v, tap, :],
                                               onehot[:, v, half * 512 + tap:half * 512 + tap + 512],
                                               start=(n == 1), stop=(n == 12))
                    mm.then_inc(s_conv, 1)
                pe.wait_ge(s_relu, b * 2 + 2)
                pe.wait_ge(s_projr, b)
                for t in range(TT):
                    mm = pe.matmul(bank[2][:, t * D:(t + 1) * D], relu[:, t // 4, (t % 4) * P:(t % 4 + 1) * P],
                                   wproj[:, :], start=True, stop=True, skip_group_check=True)
                mm.then_inc(s_proj, 1)
                norm_turn(pe, bank[3], b)
            pe.wait_ge(s_pinit, 9)
            pe.wait_ge(s_prep, 2)
            pe.wait_ge(s_xt, B)
            for i in range(8):
                before0(pe, 0, 0, i)
            recurrence(pe, rec_tensor)
            pe.wait_ge(s_keep, T // U + 1)
            pe.wait_ge(s_h[0], T)

            def fc(b):
                pe.wait_ge(s_fcr, b)
                for t in range(TT):
                    n = 0
                    for w, h in ((wfc_hi, all_hi), (wfc_lo, all_hi), (wfc_hi, all_lo)):
                        for k in range(KH):
                            n += 1
                            states = h[:, k, :, :].rearrange("p b t -> p (b t)")
                            mm = pe.matmul(bank[0][:, t * D:(t + 1) * D],
                                           states[:, bass.ds(b * T + t * P, P)], w[:, k, :],
                                           start=(n == 1), stop=(n == 6), skip_group_check=True)
                mm.then_inc(s_fc, 1)

            def on_norm(dst, w0, width, b, half):
                for part in range(3):
                    mm = pe.matmul(dst, wx[part][:, w0:w0 + width], xt[:, bass.ds(b * T + half * 512, 512)],
                                   start=(part == 0), stop=(part == 2), skip_group_check=True)
                return mm

            def on_norm_tokens(bnk, w0, width, b):
                for t in range(TT):
                    for part in range(3):
                        mm = pe.matmul(bnk[:, t * width:(t + 1) * width], xt[:, bass.ds(b * T + t * P, P)],
                                       wx[part][:, w0:w0 + width], start=(part == 0), stop=(part == 2),
                                       skip_group_check=True)
                return mm

            def ff(b):
                pe.wait_ge(s_xt, B + b + 1)
                for half in range(2):
                    for m in range(KH):
                        pe.wait_ge(s_g, b * 4 + max(0, half * 2 + m - 1))
                        on_norm(bank[2 + m][:, :], W_FF1 + m * P, P, b, half).then_inc(s_ff, 1)
                pe.wait_ge(s_g, b * 4 + 4)
                pe.wait_ge(s_yc, b)
                for m in range(KH):
                    for half in range(2):
                        mm = pe.matmul(bank[4][half * D:(half + 1) * D, :], ffw2[:, m, :], gel[:, half, m, :],
                                       start=(m == 0), stop=(m == KH - 1), skip_group_check=True)
                mm.then_inc(s_y, 1)
                pe.wait_ge(s_yc, b + 1)
                pe.wait_ge(s_ytr, b)
                for i in range(4):
                    mm = pe.transpose(bank[5][:, i * P:(i + 1) * P], yt[:, i * P:(i + 1) * P], eye[:, :])
                mm.then_inc(s_yt, 1)

            fc(0)
            norm_turn(pe, bank[1], B)
            with pe.Fori(0, B - 1) as b:
                fc(b + 1)
                ff(b)
                norm_turn(pe, bank[1], B + b + 1)
            ff(B - 1)
            if stop <= 1:
                return

            pe.wait_ge(s_wr, 1)
            pe.transpose(bank[0][0:NT, 0:P], wr[:, :], eye[:, :]).then_inc(s_wt, 1)
            for i in range(8):
                pe.wait_ge(s_enough, i + 1)
                if i == 0:
                    pe.wait_ge(s_wtc, 1)
                pe.matmul(bank[0][:, 0:1], group[:, :], enough, start=True, stop=True).then_inc(s_digit, 1)
            pe.wait_ge(s_thr, 1)
            pe.matmul(bank[0][:, 0:B], ones32[:, :], thr8, start=True, stop=True).then_inc(s_thr_all, 1)
            pe.wait_ge(s_above, 1)
            pe.matmul(bank[0][:, 64:64 + B], ones32[:, :], sum8, start=True, stop=True, skip_group_check=True)
            pe.matmul(bank[0][:, 128:192], trix[:, :], equal, start=True, stop=True, skip_group_check=True)
            pe.matmul(bank[0][:, 192:256], ones32[:, :], equal, start=True, stop=True,
                      skip_group_check=True).then_inc(s_counted, 1)

            def kq(b):
                pe.wait_ge(s_xt, 2 * B + b + 1)
                for half in range(2):
                    pe.wait_ge(s_kqg, b * 2 + half)
                    on_norm(bank[2][:, :], W_KQ1, P, b, half).then_inc(s_kq, 1)
                    if half == 0:
                        pe.wait_ge(s_vr, b)
                        on_norm_tokens(bank[6], W_V, D, b).then_inc(s_v, 1)
                    pe.wait_ge(s_kqg, b * 2 + half + 1)
                    pe.wait_ge(s_th, b * 2 + half)
                    pe.matmul(bank[4][:, :], wkq2[:, :], gel[:, half, 0, :], start=True, stop=True).then_inc(s_ph, 1)

            norm_turn(pe, bank[1], 2 * B)
            with pe.Fori(0, B - 1) as b:
                kq(b)
                norm_turn(pe, bank[1], 2 * B + b + 1)
            kq(B - 1)

            pe.wait_ge(s_vr, B)
            with pe.Fori(0, B // 2) as j:
                for q in range(2):
                    b = j * 2 + q
                    n0, m0 = b * TT, b * (TT - 1)
                    pe.wait_ge(s_phi, b + 1)

                    def scores(t):
                        pe.wait_ge(s_sm, n0 + t - 1 if t else n0)
                        pe.matmul(bank[t % 2][:, 0:P], phk[:, q, t * P:(t + 1) * P], phq[:, q, t * P:(t + 1) * P],
                                  start=True, stop=True).then_inc(s_s, 1)
                        if t + 1 < TT:
                            pe.wait_ge(s_kt, m0 + t - 1 if t else m0)
                            pe.transpose(bank[2 + t % 2][:, 0:P], phk[:, q, t * P:(t + 1) * P],
                                         eye[:, :]).then_inc(s_k, 1)

                    scores(0)
                    for t in range(TT):
                        if t + 1 < TT:
                            scores(t + 1)
                        values = vv[:, bass.ds(b * TT + t, 1), :].rearrange("p n d -> p (n d)")
                        pe.wait_ge(s_sm, n0 + t + 1)
                        if t == 0:
                            pe.wait_ge(s_rt, j * 2)
                        mm = pe.matmul(bank[4 + q][:, t * D:(t + 1) * D], sm[:, t % 2, :], values,
                                       start=True, stop=(t == 0), skip_group_check=True)
                        if t:
                            pe.wait_ge(s_stc, m0 + t)
                            mm = pe.matmul(bank[4 + q][:, t * D:(t + 1) * D], phq[:, q, t * P:(t + 1) * P], stc,
                                           start=False, stop=True, skip_group_check=True)
                        if t == 0:
                            pe.wait_ge(s_stc, m0)
                        if t + 1 < TT:
                            pe.wait_ge(s_kt, m0 + t + 1)
                            mm = pe.matmul(bank[6 + q][:, 0:D], kt[:, t % 2, :], values, start=(t == 0),
                                           stop=(t == TT - 2), skip_group_check=True)
                        mm.then_inc(s_st, 1)

            def project(b):
                pe.wait_ge(s_nrm, 3 * B + b * 2 + 1)
                pe.wait_ge(s_ntc, b)
                for i in range(4):
                    mm = pe.transpose(bank[0][:, i * P:(i + 1) * P],
                                      nrm[:, 2 * i:2 * i + 2, :].rearrange("p t d -> p (t d)"), eye[:, :])
                mm.then_inc(s_nt, 1)
                pe.wait_ge(s_ntc, b + 1)
                pe.wait_ge(s_fin, b)
                pe.wait_ge(s_wor, b)
                for i in range(4):
                    mm = pe.matmul(bank[1][:, i * P:(i + 1) * P], ntb[:, i * P:(i + 1) * P], wobd[:, :],
                                   start=True, stop=True, skip_group_check=True)
                mm.then_inc(s_wo, 1)

            def gates(b):
                norm_turn(pe, bank[3], 3 * B + b)
                pe.wait_ge(s_xt, 3 * B + b + 1)
                pe.wait_ge(s_moec, b)
                on_norm_tokens(bank[2], W_G, NE, b).then_inc(s_gt, 1)
                pe.wait_ge(s_cp, b + 1)
                for t in range(TT):
                    mm = pe.transpose(bank[3].bitcast(BF16)[:, t * P:(t + 1) * P], cp[:, t, :], eye_b[:, :])
                mm.then_inc(s_ct, 1)

            def experts(b):
                pe.wait_ge(s_ctc, b + 1)
                for part in range(3):
                    for half in range(2):
                        pe.matmul(bank[2][half * D:(half + 1) * D, :], eb2p[:, part, :],
                                  ct[:, half * 512:(half + 1) * 512], start=(part == 0), stop=False,
                                  skip_group_check=True)

                def second(e):
                    for half in range(2):
                        pe.wait_ge(s_gp, b * 16 + e * 2 + half + 1)
                        mm = pe.matmul(bank[2][half * D:(half + 1) * D, :], ew2[:, e, :], gp[:, e % 2, half, :],
                                       start=False, stop=(e == NE - 1), skip_group_check=True)
                    return mm

                for e in range(NE):
                    for half in range(2):
                        n = e * 2 + half
                        pe.wait_ge(s_r, b * 16 + max(0, n - 1))
                        on_norm(bank[4 + half][:, :], W_E1 + e * HE, HE, b, half).then_inc(s_hid, 1)
                        pe.wait_ge(s_gp, b * 16 + max(0, n - 1))
                        pe.matmul(bank[6 + half][:, :], sel16[:, e, :], ct[:, half * 512:(half + 1) * 512],
                                  start=True, stop=True).then_inc(s_c, 1)
                    if e:
                        second(e - 1)
                second(NE - 1).then_inc(s_moe, 1)
                pe.wait_ge(s_moec, b + 1)
                pe.wait_ge(s_wor, b + 1)
                for i in range(4):
                    mm = pe.transpose(bank[1][:, i * P:(i + 1) * P], yt[:, i * P:(i + 1) * P], eye[:, :])
                mm.then_inc(s_moet, 1)

            with pe.Fori(0, B) as b:
                project(b)
                gates(b)
                experts(b)

        @block.vector
        def _(dve):
            link = Chain(dve, dve_chain)

            def split2(hi, lo, src):
                link(dve.tensor_copy(hi, src))
                link(dve.tensor_tensor(lo, src, hi, ALU.subtract))

            def split3(parts, src, left):
                link(dve.tensor_copy(parts[0], src))
                link(dve.tensor_tensor(left, src, parts[0], ALU.subtract))
                link(dve.tensor_copy(parts[1], left))
                link(dve.tensor_tensor(left, left, parts[1], ALU.subtract))
                link(dve.tensor_copy(parts[2], left))

            dve.wait_ge(s_w, 16 * len(loads))
            dve.wait_ge(s_pinit, 9)
            dve.memset(embt[:, 0:1], 0.0).then_inc(s_tabw, 1)
            link(dve.tensor_reduce(stat[:, 0, 0:1], big[:, W_IH0:W_IH0 + H], AX.X, ALU.max,
                                   apply_absolute_value=True))
            for i in range(3):
                link(dve.tensor_reduce(stat[:, 0, i + 1:i + 2], wrec[:, i, :, :], AX.XY, ALU.max,
                                       apply_absolute_value=True))
            link(dve.tensor_reduce(stat[:, 5, 2:3], wfc[:, :, :], AX.XY, ALU.max, apply_absolute_value=True))
            link(dve.tensor_tensor(stat[:, 5, 0:1], stat[:, 0, 0:1], stat[:, 0, 1:2], ALU.max))
            dve.tensor_tensor(stat[:, 5, 1:2], stat[:, 0, 2:3], stat[:, 0, 3:4], ALU.max).then_inc(s_mx, 1)
            dve.wait_ge(s_mxa, 1)
            link(dve.tensor_scalar(stat[:, 7, 0:3], stat[:, 6, 0:3], 2.0 ** -100, None, ALU.max))
            link(dve.tensor_scalar(stat[:, 0, 0:3].bitcast(I32), stat[:, 7, 0:3].bitcast(I32),
                                   0x7F800000, None, ALU.bitwise_and))
            link(dve.reciprocal(stat[:, 1, 0:3], stat[:, 0, 0:3]))
            link(dve.tensor_scalar(scl[:, :], stat[:, 1, 0:3], 2.0 ** 13, None, ALU.mult))
            link(dve.tensor_scalar(inv[:, :], stat[:, 0, 0:3], 2.0 ** -13, None, ALU.mult))
            dve.tensor_scalar(big[:, W_IH0:W_IH0 + H], big[:, W_IH0:W_IH0 + H], scl[:, 0:1], None,
                              ALU.mult).then_inc(s_prep, 1)
            dve.wait_ge(s_prep, 1)
            dve.wait_ge(s_tab, 1)
            split3([t[:, :, :, :].rearrange("p a b c -> p (a b c)") for t in tab], bank[0][:, :], rest[:, 0:512])
            link(dve.tensor_copy(stat[:, 2, 0:1], stat[:, 1, 0:1]))
            dve.tensor_copy(stat[:, 3, 0:1], stat[:, 1, 0:1]).then_inc(s_tabw, 1)
            split3([w[:, :] for w in wx], big[:, :], rest[:, :])
            for i, (hi, lo, s) in enumerate(((whh_hi[0], whh_lo[0], 0), (wih1_hi, wih1_lo, 1),
                                             (whh_hi[1], whh_lo[1], 1))):
                link(dve.tensor_scalar(wrec[:, i, :, :], wrec[:, i, :, :], scl[:, s:s + 1], None, ALU.mult))
                split2(hi[:, :, :], lo[:, :, :], wrec[:, i, :, :])
            link(dve.tensor_scalar(wfc[:, :, :], wfc[:, :, :], scl[:, 2:3], None, ALU.mult))
            split2(wfc_hi[:, :, :], wfc_lo[:, :, :], wfc[:, :, :])
            for l in range(2):
                link(dve.tensor_tensor(bsum[:, l, :], brec[:, 2 * l, :], brec[:, 2 * l + 1, :], ALU.add))
                link(dve.tensor_scalar(bsum[:, l, :], bsum[:, l, :], scl[:, l:l + 1], None, ALU.mult))
            split3([eb2p[:, i, :] for i in range(3)], eb2[:, :], rest[:, 0:D])
            link(dve.tensor_copy(sel16[:, :, :], self32[:, :, :]))
            link(dve.tensor_copy(eye_b[:, :], eye[:, :]))
            link(dve.tensor_tensor(row["gb"][:, 0:NE], row["gb"][:, 0:NE], row["gb"][:, NE:2 * NE], ALU.add))
            for part in range(3):
                link(dve.tensor_copy(bpart[:, :, :], bsum[:, :, :]))
                link(dve.tensor_copy(bias[32 * part:32 * part + 1, :, :], bpart[32 * part:32 * part + 1, :, :]))
                link(dve.tensor_tensor(bsum[:, :, :], bsum[:, :, :], bpart[:, :, :], ALU.subtract))
            dve.tensor_copy(stat[:, 2, 0:1], stat[:, 1, 0:1]).then_inc(s_prep, 1)
            for i in range(4):
                dve.wait_ge(s_ids[i], 16)
            with dve.Fori(0, B) as b:
                link.loop(b, 4)
                dve.wait_ge(s_conv, b * 2)
                for v in range(2):
                    ins = dve.tensor_scalar(onehot[:, v, 1:T + 1], ids[:, bass.ds(b, 1), :].rearrange(
                        "p b t -> p (b t)"), vid[:, v:v + 1], None, ALU.is_equal)
                ins.then_inc(s_oh, 1)
                dve.wait_ge(s_proj, b + 1)
                dve.tensor_tensor(cur[:, :, :], tokens(bank[2][:, :]), rows(bproj[:, :]), ALU.add).then_inc(s_projr, 1)
                dve.wait_ge(s_projr, b + 1)
                dve.tensor_tensor(res[:, bass.ds(b * TT, TT), :], cur[:, :, :], rows(fcb[:, :]), ALU.add)
                norm_vector(dve, link, b)
                norm_split(dve, link, b)
                link.end(B)
            recurrence(dve, rec_vector)

            def halves(x):
                return x.rearrange("p (i h d) -> p h i d", i=4, h=2)

            def front(b):
                dve.wait_ge(s_fc, b + 1)
                dve.scalar_tensor_tensor(cur[:, :, :], tokens(bank[0][:, :]), inv[:, 2:3], res[:, span(b), :],
                                         ALU.mult, ALU.add).then_inc(s_fcr, 1)
                dve.wait_ge(s_fcr, b + 1)
                norm_vector(dve, link, B + b)
                norm_split(dve, link, B + b)
                dve.tensor_tensor(res[:, span(b), :], cur[:, :, :], nrm[:, :, :], ALU.add)
                link(dve.tensor_tensor(tmp8[:, :, :], nrm[:, :, :], rows(row["wr_row"][:, :]), ALU.mult))
                link(dve.reduce_sum(stat[:, 5, :], tmp8[:, :, :], AX.X))
                link(dve.tensor_scalar(wr[:, span(b)], stat[:, 5, :], column(WR_B), None, ALU.add))

            def back(b):
                dve.wait_ge(s_yt, b + 1)
                dve.tensor_tensor(tmp8[:, :, :].rearrange("p (h i) d -> p h i d", h=2), halves(bank[5][:, :]),
                                  row["ff_b2"][:, :].unsqueeze(1).unsqueeze(1).to_broadcast([P, 2, 4, D]),
                                  ALU.add).then_inc(s_ytr, 1)
                dve.wait_ge(s_ytr, b + 1)
                link(dve.tensor_tensor(yw[:, span(b), :], tmp8[:, :, :], spread(wr[:, span(b)]), ALU.mult))

            dve.wait_ge(s_fcb, 1)
            skewed(dve, front, back, link, 8)
            if stop <= 1:
                return

            dve.tensor_copy(stat[:, 2, 0:1], stat[:, 1, 0:1]).then_inc(s_wr, 1)
            link(dve.memset(key, 0))
            dve.wait_ge(s_wall, 16 * B)

            def to_float(src):
                link(dve.tensor_scalar(flip, src, 31, -1, ALU.arith_shift_right, ALU.bitwise_xor))
                link(dve.scalar_tensor_tensor(fbits, flip, -2 ** 31, src, ALU.bitwise_or, ALU.bitwise_xor))

            for i in range(8):
                shift = 28 - 4 * i
                link(dve.tensor_tensor(cand, key, digit[:, i:i + 1], ALU.bitwise_or))
                to_float(cand)
                link(dve.tensor_scalar(junk, wall, fbits.bitcast(F32), 0.0, ALU.is_ge, ALU.add, accum_out=cnt))
                dve.tensor_scalar(enough, cnt, KEEP - 0.5, None, ALU.is_ge).then_inc(s_enough, 1)
                dve.wait_ge(s_digit, i + 1)
                link(dve.tensor_copy(digi, bank[0][:, 0:1]))
                if shift:
                    link(dve.tensor_scalar(digi, digi, shift, None, ALU.logical_shift_left))
                link(dve.tensor_tensor(key, key, digi, ALU.bitwise_or))
            to_float(key)
            dve.tensor_scalar(thr8, first8[:, :], fbits.bitcast(F32), None, ALU.mult).then_inc(s_thr, 1)
            dve.wait_ge(s_thr_all, 1)
            by_seq = lambda x: x.rearrange("p (b t) -> p b t", b=B)
            over = lambda x: x.unsqueeze(2).to_broadcast([P, B, TT])
            link(dve.tensor_tensor(by_seq(above), by_seq(wr[:, :]), over(bank[0][:, 0:B]), ALU.is_gt))
            link(dve.tensor_tensor(by_seq(equal), by_seq(wr[:, :]), over(bank[0][:, 0:B]), ALU.is_equal))
            dve.reduce_sum(sum8, by_seq(above), AX.X).then_inc(s_above, 1)
            dve.wait_ge(s_counted, 1)
            link(dve.tensor_scalar(sum8, bank[0][:, 64:64 + B], -1.0, float(KEEP), ALU.mult, ALU.add))
            link(dve.memset(by_seq(offs)[:, :, 0:1], 0.0))
            for t in range(1, TT):
                link(dve.tensor_tensor(by_seq(offs)[:, :, t:t + 1], by_seq(offs)[:, :, t - 1:t],
                                       by_seq(bank[0][:, 192:256])[:, :, t - 1:t], ALU.add))
            link(dve.tensor_tensor(before, offs, bank[0][:, 128:192], ALU.add))
            link(dve.tensor_tensor(by_seq(before), by_seq(before), over(sum8), ALU.is_lt))
            link(dve.tensor_tensor(before, before, equal, ALU.mult))
            link(dve.tensor_tensor(pick[:, :], before, above, ALU.add))

            def front(b):
                link(dve.tensor_tensor(tmp8[:, :, :], yw[:, span(b), :], spread(pick[:, span(b)]), ALU.mult))
                link(dve.tensor_tensor(cur[:, :, :], tmp8[:, :, :], res[:, span(b), :], ALU.add))
                norm_vector(dve, link, 2 * B + b)
                norm_split(dve, link, 2 * B + b)
                link(dve.tensor_tensor(tmp8[:, :, :], cur[:, :, :], nrm[:, :, :], ALU.add))
                link(dve.tensor_tensor(res[:, span(b), :], tmp8[:, :, :], rows(row["bo"][:, :]), ALU.add))

            def back(b):
                dve.wait_ge(s_v, b + 1)
                dve.tensor_tensor(vv[:, span(b), :], tokens(bank[6][:, :]), rows(row["bv"][:, :]),
                                  ALU.add).then_inc(s_vr, 1)
                for half in range(2):
                    dve.wait_ge(s_thr_r, b * 2 + half)
                    dve.wait_ge(s_th, b * 2 + half + 1)
                    link(dve.tensor_scalar(turns[:, :], th[:, half, :], column(TURN + 2), None, ALU.mult))
                    link(dve.tensor_scalar(whole[:, :], turns[:, :], MAGIC, -MAGIC, ALU.add, ALU.add))
                    dve.tensor_tensor(rph[:, bass.ds(b * T + half * 512, 512)], turns[:, :], whole[:, :],
                                      ALU.subtract).then_inc(s_thr_r, 1)

            skewed(dve, front, back, link, 12)

            with dve.Fori(0, B // 2) as j:
                for q in range(2):
                    b = j * 2 + q
                    n0, m0 = b * TT, b * (TT - 1)

                    def evacuate(t):
                        dve.wait_ge(s_s, n0 + t + 1)
                        dve.tensor_tensor(sm[:, t % 2, :], bank[t % 2][:, 0:P], tri[:, :], ALU.mult).then_inc(s_sm, 1)
                        if t + 1 < TT:
                            dve.wait_ge(s_k, m0 + t + 1)
                            dve.tensor_copy(kt[:, t % 2, :], bank[2 + t % 2][:, 0:P]).then_inc(s_kt, 1)

                    evacuate(0)
                    for t in range(TT):
                        dve.wait_ge(s_st, n0 + t + 1)
                        if t + 1 < TT:
                            dve.tensor_copy(stc, bank[6 + q][:, 0:D]).then_inc(s_stc, 1)
                            evacuate(t + 1)
                    dve.tensor_tensor(yw[:, span(b), :], tokens(bank[4 + q][:, :]), spread(posr[:, :]),
                                      ALU.mult).then_inc(s_rt, 1)
            dve.wait_ge(s_rt, B)

            def front(b):
                link(dve.tensor_scalar(cur[:, :, :], yw[:, span(b), :], 1.0, None, ALU.mult))
                norm_vector(dve, link, 3 * B + b * 2)
                dve.wait_ge(s_wo, b + 1)
                dve.tensor_tensor(cur[:, :, :], tokens(bank[1][:, :]), res[:, span(b), :], ALU.add).then_inc(s_wor, 1)
                dve.wait_ge(s_wor, b + 1)
                norm_vector(dve, link, 3 * B + b * 2 + 1)
                norm_split(dve, link, 3 * B + b)
                dve.tensor_scalar(res[:, span(b), :], cur[:, :, :], 1.0, None, ALU.mult)
                dve.wait_ge(s_gt, b + 1)
                link(dve.tensor_tensor(lg[:, :, :], bank[2][:, 0:TT * NE].rearrange("p (t e) -> p t e", t=TT),
                                       row["gb"][:, 0:NE].unsqueeze(1).to_broadcast([P, TT, NE]), ALU.add))
                link(dve.tensor_reduce(stat[:, 5, :], lg[:, :, :], AX.X, ALU.max))
                per = lambda x: x.unsqueeze(2).to_broadcast([P, TT, NE])
                dve.tensor_tensor(gc[:, :, :], lg[:, :, :], per(stat[:, 5, :]), ALU.subtract).then_inc(s_lm, 1)
                link(dve.tensor_tensor(gdiff[:, :, :, :], lg[:, :, :].unsqueeze(2).to_broadcast([P, TT, NE, NE]),
                                       lg[:, :, :].unsqueeze(3).to_broadcast([P, TT, NE, NE]), ALU.subtract))
                link(dve.tensor_tensor(gdiff[:, :, :, :], gdiff[:, :, :, :],
                                       order[:, :, :].unsqueeze(1).to_broadcast([P, TT, NE, NE]), ALU.is_gt))
                link(dve.reduce_sum(grank[:, :, :], gdiff[:, :, :, :], AX.X))
                link(dve.tensor_scalar(gsel[:, :, :], grank[:, :, :], 1.5, None, ALU.is_lt))
                dve.wait_ge(s_ex, b + 1)
                link(dve.tensor_tensor(gc[:, :, :], gex[:, :, :], gsel[:, :, :], ALU.mult))
                link(dve.reduce_sum(stat[:, 6, :], gc[:, :, :], AX.X))
                link(dve.reciprocal(stat[:, 7, :], stat[:, 6, :]))
                link(dve.tensor_tensor(gleft[:, :, :], gc[:, :, :], per(stat[:, 7, :]), ALU.mult))
                dve.wait_ge(s_ct, b)
                link(dve.tensor_copy(cp[:, :, 0:NE], gleft[:, :, :]))
                link(dve.tensor_tensor(gleft[:, :, :], gleft[:, :, :], cp[:, :, 0:NE], ALU.subtract))
                link(dve.tensor_copy(cp[:, :, NE:2 * NE], gleft[:, :, :]))
                link(dve.tensor_tensor(gleft[:, :, :], gleft[:, :, :], cp[:, :, NE:2 * NE], ALU.subtract))
                dve.tensor_copy(cp[:, :, 2 * NE:3 * NE], gleft[:, :, :]).then_inc(s_cp, 1)

            def back(b):
                for e in range(NE):
                    for half in range(2):
                        n = b * 16 + e * 2 + half
                        dve.wait_ge(s_r, n + 1)
                        dve.wait_ge(s_c, n + 1)
                        dve.tensor_tensor(gp[:, e % 2, half, :], gr[:, e % 2, half, :], bank[6 + half][:, :],
                                          ALU.mult).then_inc(s_gp, 1)
                dve.wait_ge(s_moet, b + 1)
                own = res[:, span(b), :].rearrange("p (h i) d -> p h i d", h=2)
                dve.tensor_tensor(own, halves(bank[1][:, :]), own, ALU.add).then_inc(s_fin, 1)

            with dve.Fori(0, B) as b:
                link.loop(b, 22)
                front(b)
                back(b)
                link.end(B)


def lay_out(inp):
    f = lambda n: np.ascontiguousarray(inp[n])
    twice = lambda w: np.concatenate([w, w], 0)
    conv = f("L0_tok_conv_w")
    wconv = np.zeros((P, 2, P), conv.dtype)
    for g in range(P // 8):
        for tap in range(2):
            wconv[g * 8:g * 8 + 8, tap, g * 8:g * 8 + 8] = conv[g * 8:g * 8 + 8, :, tap].T
    tiles = lambda w: w.T.reshape(KH, P, -1).transpose(1, 0, 2)
    wx = np.concatenate([
        f("L0_attn_W_ih_0").T, f("L0_ffn_w1"), f("L1_attn_Wk1"), f("L1_attn_Wq1"), f("L1_attn_Wv"),
        f("L1_ffn_Wg"), f("L1_ffn_W1").transpose(1, 0, 2).reshape(D, NE * HE)], 1)
    z = lambda *shape: np.zeros(shape, np.float32)
    col = z(P, 16)
    col[:, 0:2] = f("L0_ffn_b1").reshape(KH, P).T
    for i, (k, q) in ((2, ("bk1", "bq1")), (3, ("bk2", "bq2")), (4, ("ln_w", "ln_w")), (5, ("ln_b", "ln_b"))):
        col[:D, i], col[D:, i] = f("L1_attn_" + k), f("L1_attn_" + q)
    col[:, 6] = np.pi / 2
    col[:, 7] = f("L0_ffn_br")[0]
    col[:, 8] = np.tile(np.repeat(2.0 ** np.arange(4), 16), 2) / 2
    wkq2, wobd = z(P, P), z(P, P)
    wkq2[:D, :D], wkq2[D:, D:] = f("L1_attn_Wk2"), f("L1_attn_Wq2")
    wobd[:D, :D] = wobd[D:, D:] = f("L1_attn_Wo")
    eb2, select = z(P, D), z(P, NE, P)
    for part in range(3):
        eb2[part * NE:part * NE + NE] = f("L1_ffn_b2")
        for e in range(NE):
            select[part * NE + e, e] = 1
    p = np.arange(P)
    group = ((p[:, None] // 16 == p // 16) & (p[:, None] % 16 > 0)).astype(np.float32)
    first8 = (p[:, None] == 16 * np.arange(B)).astype(np.float32)
    digit = ((p[:, None] % 16).astype(np.int64) << (28 - 4 * np.arange(8))).astype(np.uint32).view(np.int32)
    digit[::16, 0] = -2 ** 31
    posr = (1.0 / np.sqrt((p[:, None] + P * np.arange(TT) + 1.0) * D)).astype(np.float32)
    e = np.arange(NE)
    order = np.where(e < e[:, None], -1e-37, np.where(e == e[:, None], 1.0, 0.0)).astype(np.float32)
    a = {
        "x": f("x"),
        "wx": twice(wx),
        "wrec": np.stack([tiles(f(n)) for n in ("L0_attn_W_hh_0", "L0_attn_W_ih_1", "L0_attn_W_hh_1")], 1),
        "wfc": tiles(f("L0_attn_fc_w")),
        "brec": np.concatenate([f(n) for n in ("L0_attn_b_ih_0", "L0_attn_b_hh_0", "L0_attn_b_ih_1",
                                               "L0_attn_b_hh_1")]),
        "embt": f("L0_tok_embed_table").T,
        "wconv": wconv,
        "wproj": f("L0_tok_proj_w").T,
        "proj_b": f("L0_tok_proj_b"),
        "fc_b": f("L0_attn_fc_b"),
        "wr_row": f("L0_ffn_wr")[:, 0],
        "bo": f("L1_attn_bo"), "bv": f("L1_attn_bv"), "ff_b2": f("L0_ffn_b2"),
        "gb": np.concatenate([f("L1_ffn_bg"), f("L1_ffn_bias")]),
        "col": col, "ebias": f("L1_ffn_b1").T, "ffw2": f("L0_ffn_w2").reshape(KH, P, D).transpose(1, 0, 2),
        "wkq2": wkq2, "wobd": wobd, "ew2": f("L1_ffn_W2").transpose(1, 0, 2), "eb2": eb2, "self32": select,
        "tri": np.triu(np.ones((P, P), np.float32)), "trix": np.triu(np.ones((P, P), np.float32), 1),
        "group": group, "first8": first8, "digit": digit,
        "posr": posr, "order": np.broadcast_to(order, (P, NE, NE)),
        "vid": np.arange(VOC, dtype=np.float32).reshape(2, P).T,
        "eye": np.eye(P, dtype=np.float32),
        "eye16": np.eye(P, dtype=np.float16),
    }
    return {k: np.ascontiguousarray(v) for k, v in a.items()}


def kernel(**inputs):
    import concourse.bacc as bacc
    from concourse.bass_utils import run_bass_kernel_spmd

    nc = bacc.Bacc("TRN2", target_bir_lowering=False, num_devices=1)
    arrays = {f"in_{k}": v for k, v in lay_out(inputs).items()}
    args = {k[3:]: nc.dram_tensor(k, v.shape, mybir.dt.from_np(v.dtype), kind="ExternalInput").ap()
            for k, v in arrays.items()}
    out = nc.dram_tensor("out", (B, T, D), F32, kind="ExternalOutput").ap()
    build(nc, args, out)
    r = run_bass_kernel_spmd(nc, [arrays], core_ids=[0])
    return r.results[0]["out"]
```

```python
from contextlib import ExitStack

import numpy as np

import concourse.bass as bass
from concourse import mybir

ALU = mybir.AluOpType
ACT = mybir.ActivationFunctionType
F32 = mybir.dt.float32
F16 = mybir.dt.float16
BF16 = mybir.dt.bfloat16
I32 = mybir.dt.int32
AX = mybir.AxisListType
RMAX = bass.bass_isa.ReduceOp.max

P = 128
KEEP = 511
B, T = 8, 1024
D = 64
H = 256
KH = H // P
TT = T // P
NT = B * TT
VOC = 256
NE, HE = 8, 128
U = 32
LAG = 20
OFF = U + LAG
BODY = 2 * U
EPS = 1e-5
TWO_PI = 2.0 * np.pi
MAGIC = 1.5 * 2.0 ** 23

W_FF1, W_KQ1, W_V, W_G, W_E1, W_WR, W_END = W_AT = 0, 256, 384, 448, 456, 1480, 1481
S_L0, S_L1, S_FC, S_FF1, S_KQ1, S_V, S_G, S_E1, S_WR, S_END = range(10)


OPEN = 1
NORMS = 5


class Chain:

    def __init__(self, eng, sem):
        self.eng, self.sem, self.base, self.n, self.i, self.per = eng, sem, 0, 0, None, 0

    def __call__(self, ins):
        ins.then_inc(self.sem, 1)
        self.n += 1
        at = self.base + self.n
        self.eng.wait_ge(self.sem, at if self.i is None else self.i * self.per + at)

    def loop(self, i, per):
        self.base, self.n, self.i, self.per = self.base + self.n, 0, i, per

    def end(self, count):
        assert self.n == self.per, (self.n, self.per)
        self.base, self.n, self.i = self.base + self.per * count, 0, None


def build(nc, a, out):
    with ExitStack() as ctx:
        def sb(name, shape, dt=F32):
            return ctx.enter_context(nc.sbuf_tensor(name, shape, dt))

        def sem(name):
            return ctx.enter_context(nc.semaphore(name))

        bank = [ctx.enter_context(nc.psum_tensor(f"bank{i}", [P, 512], F32)) for i in range(8)]

        def sums(layer, block, step):
            own = bank[layer * 4 + block % 2 * 2 + step % 2]
            return own[:, 0:U * B].rearrange("p (m s b) -> p m s b", m=KH, b=B)

        res = sb("res", [P, NT, D])
        yw = sb("yw", [P, NT, D])
        wr = sb("wr", [P, NT])
        pick = sb("pick", [P, NT])
        xt = sb("xt", [P, B * T], F16)
        xr = sb("xr", [P, T, B], F16)
        all_hi = sb("all_hi", [P, KH, B, T], F16)
        all_lo = sb("all_lo", [P, KH, B, T], F16)
        eye = sb("eye", [P, P])
        eye16 = sb("eye16", [P, P], F16)
        wx = [sb(f"wx{i}", [P, W_END], F16) for i in range(2)]
        whh_hi = [sb(f"whh{l}_hi", [P, KH, H], F16) for l in range(2)]
        whh_lo = [sb(f"whh{l}_lo", [P, KH, H], F16) for l in range(2)]
        wih1_hi = sb("wih1_hi", [P, KH, H], F16)
        wih1_lo = sb("wih1_lo", [P, KH, H], F16)
        wfc_hi = sb("wfc_hi", [P, KH, D], F16)
        wfc_lo = sb("wfc_lo", [P, KH, D], F16)
        wih0_hi = sb("wih0_hi", [P, H], F16)
        wih0_lo = sb("wih0_lo", [P, H], F16)
        bias = sb("bias", [P, 2 * H + 2 * D], BF16)
        B_O, B_V = 2 * H, 2 * H + D
        warm = sb("warm", [P, 1])
        ones = sb("ones", [P, P], BF16)
        scl = sb("scl", [P, S_END])
        inv = sb("inv", [P, S_END])
        stat = sb("stat", [P, 8, 8])
        fcb = sb("fcb", [P, D])
        cur = sb("cur", [P, TT, D])
        nrm = sb("nrm", [P, TT, D])
        xc = sb("xc", [P, TT, D])
        sq = sb("sq", [P, TT, D])
        tmp8 = sb("tmp8", [P, TT, D])
        xs = sb("xs", [P, TT, 2, D], F16)
        nhalf = sb("nhalf", [P, TT])
        start = sb("start", [1, 64])

        s_w = [sem(f"group{i}_loaded") for i in range(3)]
        s_ids = [sem(f"ids_loaded{i}") for i in range(4)]
        s_out = sem("out_written")
        dve_chain, act_chain, pool_chain = sem("dve_order"), sem("act_order"), sem("pool_order")

        s_mx = sem("largest_weights")
        s_mxa = sem("largest_weights_all")
        s_tab = sem("table_summed")
        s_tabw = sem("table_split")
        s_prep = sem("weights_ready")
        s_pinit = sem("pool_constants")
        s_oh = sem("onehot_ready")
        s_conv = sem("conv_summed")
        s_relu = sem("conv_relu")
        s_proj = sem("proj_summed")
        s_projr = sem("proj_read")
        s_nrm = sem("normalised")
        s_xc, s_sq, s_var, s_rstd, s_xh, s_xs, s_tr, s_xt = (
            sem(n) for n in ("centred", "squared", "variance", "rstd", "norm_high", "norm_split", "norm_turned", "norm_copied"))
        s_sum = [sem("sum0_ready"), sem("sum1_ready")]
        s_hi = [sem("state0_high"), sem("state1_high")]
        s_h = [sem("state0_ready"), sem("state1_ready")]
        s_lo = [sem("state0_low"), sem("state1_low")]
        s_keep = sem("state1_kept")
        s_fc = sem("fc_summed")
        s_fcr = sem("fc_read")
        
        s_fcb = sem("pool_tail")
        s_ff, s_g, s_y, s_yc, s_yt, s_ytr, s_rw = (
            sem(n) for n in ("ff_hidden", "ff_gelu", "ff_summed", "ff_copied", "ff_turned", "ff_kept", "router_summed"))
        s_wr, s_wt, s_wtc, s_wdram, s_wall, s_enough, s_digit = (
            sem(n) for n in ("router_ready", "router_turned", "router_copied", "router_in_dram", "router_spread",
                             "enough_above", "digit_counted"))
        s_thr, s_thr_all, s_above, s_counted = (
            sem(n) for n in ("threshold", "threshold_spread", "above_ready", "above_counted"))
        s_kq, s_kqg, s_ph, s_th, s_thr_r, s_v, s_vr = (
            sem(n) for n in ("kq_hidden", "kq_gelu", "kq_phase", "kq_tanh", "phase_kept", "values_summed", "values_kept"))
        s_phk, s_phi, s_s, s_sm, s_k, s_kt, s_st, s_mem, s_att, s_rt = (
            sem(n) for n in ("key_phasors", "phasors", "scores", "scores_masked", "keys_turned", "keys_copied",
                             "memory_added", "memory_summed", "attention_summed", "attention_kept"))
        s_nt, s_ntc, s_wo, s_wor = (sem(n) for n in ("att_turned", "att_scaled", "att_projected", "att_added"))
        s_gt, s_lg, s_rank, s_lm, s_ex, s_cp, s_ct, s_ctc = (
            sem(n) for n in ("gates_summed", "gates_biased", "gates_compared", "gates_shifted", "gates_exp", "weights_split", "weights_turned",
                             "weights_copied"))
        s_hid, s_r, s_c, s_gp, s_moe, s_moec, s_moet, s_fin = (
            sem(n) for n in ("expert_hidden", "expert_relu", "expert_weight", "expert_weighted", "experts_summed",
                             "experts_copied", "experts_turned", "sequence_done"))

        opened = (*s_hi, *s_lo, s_tr, s_xt, s_xs, s_keep, s_proj, s_projr, s_relu, s_conv, s_fcr, s_y, s_yt, s_yc,
                  s_ytr, s_g, s_ph, s_thr_r, s_kqg, s_vr, s_th, s_c, s_gp, s_moet, s_moec, s_lm, s_r, s_fin, s_ct)

        gate_bias = sb("gate_bias", [P, 2 * NE])
        col = sb("col", [P, 16])
        ebias = sb("ebias", [P, NE])
        ffw2 = sb("ffw2", [P, KH, D])
        wkq2 = sb("wkq2", [P, P])
        wobd = sb("wobd", [P, P])
        ew2 = sb("ew2", [P, NE, D])
        eb2 = sb("eb2", [P, D])
        eb2p = sb("eb2p", [P, 3, D], BF16)
        self32 = sb("self32", [P, NE, P])
        sel16 = sb("sel16", [P, NE, P], F16)
        tri = sb("tri", [P, P])
        trix = sb("trix", [P, P])
        ones32 = sb("ones32", [P, P])
        group = sb("group", [P, P])
        first8 = sb("first8", [P, B])
        digit = sb("digit", [P, 8], I32)
        posr = sb("posr", [P, TT])
        order = sb("order", [P, NE, NE])
        router_dram = nc.dram_tensor("router_dram", (B, T), F32, kind="Internal").ap()

        ph = ExitStack()

        def tmp(name, shape, dt=F32):
            return ph.enter_context(nc.sbuf_tensor(name, shape, dt))

        lo_space = all_lo[:, :, :, :].rearrange("p k b t -> p (k b t)").bitcast(F32)
        hi_space = all_hi[:, :, :, :].rearrange("p k b t -> p (k b t)")
        big = lo_space[:, 0:W_END]
        rest = lo_space[:, W_END:2 * W_END]
        wrec = lo_space[:, 2 * W_END:2 * W_END + 3 * KH * H].rearrange("p (i k h) -> p i k h", i=3, k=KH)
        wfc = tmp("wfc", [P, KH, D])
        wih0 = tmp("wih0", [P, H])
        brec = tmp("brec", [P, 4, H])
        bsum = tmp("bsum", [P, 2 * H + 2 * D])
        bpart = tmp("bpart", [P, 2 * H + 2 * D], BF16)
        embt = tmp("embt", [P, VOC])
        wconv = tmp("wconv", [P, 2, P])
        tab = [tmp(f"tab{i}", [P, 2, 2, P], BF16) for i in range(3)]
        wproj = tmp("wproj", [P, D])
        bproj = tmp("bproj", [P, D])
        vid = tmp("vid", [P, 2])
        ids = hi_space.bitcast(I32).rearrange("p (b t) -> p b t", b=B)
        onehot = tmp("onehot", [P, 2, T + 2], BF16)
        left512 = tmp("left512", [P, 512])
        relu = tmp("relu", [P, 2, 512])
        h_hi = [tmp(f"h{l}_hi", [P, 2, KH, U, B], F16) for l in range(2)]
        h_lo = [tmp(f"h{l}_lo", [P, 2, KH, U, B], F16) for l in range(2)]
        h_f = [tmp(f"h{l}_f", [P, 2, KH, B]) for l in range(2)]

        loads = [
            [(embt[:, :], a["embt"]), (wconv[:, :, :], a["wconv"]), (vid[:, :], a["vid"])],
            [(wrec[:, :, :, :], a["wrec"]), (wfc[:, :, :], a["wfc"]), (wih0[:, :], a["wih0"]),
             (wproj[:, :], a["wproj"]), (bproj[:, :], a["proj_b"].partition_broadcast(P)),
             (fcb[:, :], a["fc_b"].partition_broadcast(P)), (eye16[:, :], a["eye16"]),
             (brec[:, :, :].rearrange("p a h -> p (a h)"), a["brec"].partition_broadcast(P)),
             (bsum[:, B_O:B_O + 2 * D], a["bov"].partition_broadcast(P))],
            [(big[:, :], a["wx"]), (gate_bias[:, :], a["gb"].partition_broadcast(P)),
             (col[:, :], a["col"]), (ebias[:, :], a["ebias"]), (ffw2[:, :, :], a["ffw2"]), (wkq2[:, :], a["wkq2"]),
             (wobd[:, :], a["wobd"]), (ew2[:, :, :], a["ew2"]), (eb2[:, :], a["eb2"]),
             (self32[:, :, :], a["self32"]), (tri[:, :], a["tri"]), (trix[:, :], a["trix"]),
             (group[:, :], a["group"]), (first8[:, :], a["first8"]), (digit[:, :], a["digit"]),
             (posr[:, :], a["posr"]), (order[:, :, :], a["order"]), (eye[:, :], a["eye"])],
        ]

        def spread(x):
            return x.unsqueeze(2).to_broadcast([P, TT, D])

        def rows(x):
            return x.unsqueeze(1).to_broadcast([P, TT, D])

        def tokens(x):
            return x.rearrange("p (t d) -> p t d", t=TT)

        def norm_centre(dve, link):
            link(dve.reduce_sum(stat[:, 0, :], cur[:, :, :], AX.X))
            link(dve.tensor_scalar(stat[:, 1, :], stat[:, 0, :], 1.0 / D, None, ALU.mult))
            dve.tensor_tensor(xc[:, :, :], cur[:, :, :], spread(stat[:, 1, :]), ALU.subtract).then_inc(s_xc, 1)

        def norm_variance(dve, link, k):
            dve.wait_ge(s_sq, k + 1)
            link(dve.reduce_sum(stat[:, 2, :], sq[:, :, :], AX.X))
            dve.tensor_scalar(stat[:, 3, :], stat[:, 2, :], 1.0 / D, EPS, ALU.mult, ALU.add).then_inc(s_var, 1)

        def norm_scale(dve, k):
            dve.wait_ge(s_rstd, k + 1)
            dve.tensor_tensor(nrm[:, :, :], xc[:, :, :], spread(stat[:, 4, :]), ALU.mult).then_inc(s_nrm, 1)

        def norm_vector(dve, link, k):
            norm_centre(dve, link)
            norm_variance(dve, link, k)
            norm_scale(dve, k)
            dve.wait_ge(s_nrm, k + 1)

        def norm_high(act, n, k):
            act.wait_ge(s_nrm, n + 1)
            act.wait_ge(s_tr, OPEN + k)
            act.activation(xs[:, :, 0, :], nrm[:, :, :], ACT.Copy).then_inc(s_xh, 1)

        def norm_low(dve, k):
            dve.wait_ge(s_xh, k + 1)
            dve.tensor_tensor(xs[:, :, 1, :], nrm[:, :, :], xs[:, :, 0, :], ALU.subtract).then_inc(s_xs, 1)

        def norm_square(act, k):
            act.wait_ge(s_xc, k + 1)
            act.activation(sq[:, :, :], xc[:, :, :], ACT.Square).then_inc(s_sq, 1)

        def norm_rstd(pool, k):
            pool.wait_ge(s_var, k + 1)
            pool.tensor_tensor(stat[:, 4, :], stat[:, 3, :], nhalf[:, :], ALU.pow).then_inc(s_rstd, 1)

        def norm_turn(pe, dst, k):
            pe.wait_ge(s_xs, OPEN + k + 1)
            pe.wait_ge(s_xt, OPEN + k)
            for t in range(TT):
                mm = pe.transpose(dst.bitcast(F16)[:, t * P:(t + 1) * P],
                                  xs[:, t, :, :].rearrange("p a d -> p (a d)"), eye16[:, :])
            mm.then_inc(s_tr, 1)

        def norm_copy(act, dst, src, k):
            act.wait_ge(s_tr, OPEN + k + 1)
            act.activation(dst, src.bitcast(F16)[:, 0:T], ACT.Copy).then_inc(s_xt, 1)

        def rec_tensor(pe, g, j, l0, l1):
            def step(layer, s):
                u = s % U
                pq, pu = ((s - 1) // U) % 2, (s - 1) % U
                at = j * BODY + s
                own = sums(layer, s // U, s)
                pe.wait_ge(s_hi[layer], OPEN + at)
                for w in (whh_hi, whh_lo):
                    for m in range(KH):
                        for k in range(KH):
                            pe.matmul(own[:, m, u // 2, :], w[layer][:, k, m * P:(m + 1) * P],
                                      h_hi[layer][:, pq, k, pu, :], start=False, stop=False,
                                      skip_group_check=True)
                pe.wait_ge(s_lo[layer], OPEN + at)
                for m in range(KH):
                    for k in range(KH):
                        mm = pe.matmul(own[:, m, u // 2, :], whh_hi[layer][:, k, m * P:(m + 1) * P],
                                       h_lo[layer][:, pq, k, pu, :], start=False, stop=False,
                                       skip_group_check=True)
                mm.then_inc(s_sum[layer], 1)

            if l0:
                step(0, g)
            u, block = g % U, g // U
            if u >= LAG and block + 1 < T // U:
                before0(pe, block + 1, j, u - LAG)
            if 1 <= block <= T // U and u < LAG:
                for i in range(28 * u // LAG, 28 * (u + 1) // LAG):
                    before1(pe, block - 1, i)
            if l1:
                step(1, g - OFF)

        def before0(pe, n, j, i):
            odd, m, part = i // 6, i // 3 % 2, i % 3
            own = sums(0, n, odd)[:, m, :, :]
            if part == 0:
                pe.matmul(own, bias[:, m * P:(m + 1) * P], ones[:, :], start=(m == 0), stop=False,
                          skip_group_check=True)
            else:
                x = xr[:, :, :].rearrange("p (t two) b -> p two t b", two=2)[:, odd, :, :]
                pe.matmul(own, (wih0_hi, wih0_lo)[part - 1][:, m * P:(m + 1) * P],
                          x[:, bass.ds(j * (BODY // 2) + n * U // 2, U // 2), :],
                          start=False, stop=False, skip_group_check=True)

        def before1(pe, n, i):
            odd, m, part = i // 14, i // 7 % 2, i % 7
            own = sums(1, n, odd)[:, m, :, :]
            if part == 0:
                pe.matmul(own, bias[:, H + m * P:H + (m + 1) * P], ones[:, :], start=(m == 0), stop=False,
                          skip_group_check=True)
            else:
                w, h = ((wih1_hi, h_hi), (wih1_lo, h_hi), (wih1_hi, h_lo))[(part - 1) // 2]
                k = (part - 1) % 2
                pe.matmul(own, w[:, k, m * P:(m + 1) * P],
                          h[0][:, n % 2, k, :, :].rearrange("p (s two) b -> p two s b", two=2)[:, odd, :, :],
                          start=False, stop=False, skip_group_check=True)

        def rec_scalar(act, g, j, l0, l1, scale):
            for layer, on, s in ((0, l0, g), (1, l1, g - OFF)):
                if not on:
                    continue
                q, u = (s // U) % 2, s % U
                if layer == 1 and u == 0:
                    act.wait_ge(s_keep, OPEN + j * 2 + s // U)
                own = sums(layer, s // U, s)[:, :, u // 2, :]
                act.wait_ge(s_sum[layer], j * BODY + s + 1)
                act.activation(h_hi[layer][:, q, :, u, :], own, ACT.Tanh, scale=scale[layer]).then_inc(s_hi[layer], 1)
                act.activation(h_f[layer][:, s % 2, :, :], own, ACT.Tanh,
                               scale=scale[layer]).then_inc(s_h[layer], 1)

        def rec_vector(dve, g, j, l0, l1):
            for layer, on, s in ((0, l0, g), (1, l1, g - OFF)):
                if not on:
                    continue
                q, u = (s // U) % 2, s % U
                dve.wait_ge(s_h[layer], j * BODY + s + 1)
                dve.tensor_tensor(h_lo[layer][:, q, :, u, :], h_f[layer][:, s % 2, :, :],
                                  h_hi[layer][:, q, :, u, :], ALU.subtract).then_inc(s_lo[layer], 1)

        def recurrence(eng, slot):
            count = (T - OFF) // BODY
            for g in range(OFF):
                slot(eng, g, 0, True, False)
            with eng.Fori(0, count) as j:
                for g in range(OFF, OFF + BODY):
                    slot(eng, g, j, True, True)
            for g in range(OFF + BODY * count, T + OFF):
                slot(eng, g, 0, g < T, True)

        ph.close()
        ph = ctx.enter_context(ExitStack())
        rph = hi_space.bitcast(F32)
        vv = xr[:, :, :].rearrange("p t b -> p (t b)").bitcast(F32).rearrange("p (n d) -> p n d", d=D)
        gel = tmp("gel", [P, 2, KH, 512])
        yt = tmp("yt", [P, 512])
        th = tmp("th", [P, 2, 512])
        turns = tmp("turns", [P, 512])
        whole = tmp("whole", [P, 512])
        lo2 = lo_space
        wall = lo2[:, 0:T]
        junk = lo2[:, T:T + 512].bitcast(BF16)
        wt = lo2[:, 1536:1536 + P]
        above, equal, before, offs = (lo2[:, 1700 + 64 * i:1764 + 64 * i] for i in range(4))
        key, cand, flip, fbits, digi = (lo2[:, 2000 + i:2001 + i].bitcast(I32) for i in range(5))
        cnt, enough = (lo2[:, 2010 + i:2011 + i] for i in range(2))
        thr8, sum8 = (lo2[:, 2020 + 8 * i:2028 + 8 * i] for i in range(2))
        rabs = lo2[:, 2048:3072]
        phk, phq = (lo2[:, 3072 + 2048 * i:3072 + 2048 * (i + 1)].rearrange("p (q t) -> p q t", q=2) for i in range(2))
        gp = tmp("gp", [P, 2, 2, 512])
        kt = lo2[:, 7168:8192].rearrange("p (t k) -> p t k", t=TT)
        sm = gel[:, :, :, :].rearrange("p a b (t k) -> p a (b t) k", k=P)
        mem = gp[:, :, :, :].rearrange("p a b (t d) -> p (a b t) d", d=D)[:, 2 * TT:3 * TT, :]
        ntb = turns
        lg, gex = tmp("lg", [P, TT, NE]), tmp("gex", [P, TT, NE])
        gdiff = tmp("gdiff", [P, TT, NE, NE])
        grank, gsel, gc, gleft = (tmp(n, [P, TT, NE]) for n in ("grank", "gsel", "gc", "gleft"))
        cp = tmp("cp", [P, TT, P], F16)
        ct = tmp("ct", [P, T], F16)
        gr = gel

        def skewed(eng, front, back, link=None, links=0, last=lambda b: None):
            front(0)
            last(0)
            with eng.Fori(0, B - 1) as b:
                if link:
                    link.loop(b, links)
                front(b + 1)
                back(b)
                last(b + 1)
                if link:
                    link.end(B - 1)
            back(B - 1)

        def attention(eng, step, link=None, links=0):
            for n in (-1, 0):
                step(n, n)
            with eng.Fori(0, (B - 4) // 2) as j:
                if link:
                    link.loop(j, links)
                for n in (1, 2):
                    step(n, j * 2 + n)
                if link:
                    link.end((B - 4) // 2)
            for n in range(B - 3, B + 1):
                step(n, n)

        def experts(eng, gate_part, weights, expert, finish, link=None, links=0, before=NE):
            for e in range(NE):
                gate_part(0, e)
            weights(0)
            with eng.Fori(0, B - 1) as b:
                if link:
                    link.loop(b, links)
                for e in range(NE):
                    if e >= before:
                        gate_part(b + 1, e)
                    expert(b, e)
                    if e < before:
                        gate_part(b + 1, e)
                weights(b + 1)
                finish(b, True)
                if link:
                    link.end(B - 1)
            for e in range(NE):
                expert(B - 1, e)
            finish(B - 1, False)

        FF_B1, KQ_B1, KQ_B2, LN_W, LN_B, QUARTER, WR_B, TURNS, FF_B2 = 0, 2, 3, 4, 5, 6, 7, 8, 9
        column = lambda i: col[:, i:i + 1]
        span = lambda b: bass.ds(b * TT, TT)

        block = ctx.enter_context(nc.Block())

        @block.sync
        def _(sp):
            for g in range(3):
                for dst, src in loads[g]:
                    sp.dma_start(dst, src).then_inc(s_w[g], 16)
                for i in ((0,), (1, 2, 3), ())[g]:
                    sp.dma_start(ids[:, 2 * i:2 * i + 2, :],
                                 a["x"][2 * i:2 * i + 2, :].partition_broadcast(P)).then_inc(s_ids[i], 16)
            sp.wait_ge(s_wtc, 1)
            sp.dma_start(router_dram.rearrange("b (t p) -> (b t) p", p=P), wt[0:NT, :]).then_inc(s_wdram, 16)
            sp.wait_ge(s_wdram, 16)
            for b in range(B):
                sp.dma_start(wall[b * 16:b * 16 + 16, :],
                             router_dram[b:b + 1, :].partition_broadcast(16)).then_inc(s_wall, 16)
            for b in range(B):
                sp.wait_ge(s_fin, OPEN + b + 1)
                sp.dma_start(out[b].rearrange("(t p) d -> p t d", p=P),
                             res[:, b * TT:(b + 1) * TT, :]).then_inc(s_out, 16)
            sp.wait_ge(s_out, 16 * B)

        @block.gpsimd
        def _(pool):
            for i, s in enumerate(opened):
                pool.memset(start[0:1, i:i + 1], 0.0).then_inc(s, OPEN)
            pool.memset(nhalf[:, :], -0.5).then_inc(s_pinit, 1)
            for l in range(2):
                pool.memset(h_hi[l][:, 1, :, U - 1, :], 0.0).then_inc(s_pinit, 1)
                pool.memset(h_lo[l][:, 1, :, U - 1, :], 0.0).then_inc(s_pinit, 1)
            pool.memset(ones[:, :], 1.0).then_inc(s_pinit, 1)
            pool.memset(bias[:, :], 0.0).then_inc(s_pinit, 1)
            pool.memset(onehot[:, :, 0:1], 0.0).then_inc(s_pinit, 1)
            pool.memset(stat[:, 5, 7:8], 0.0).then_inc(s_keep, 1)
            pool.memset(ones32[:, :], 1.0).then_inc(s_pinit, 1)
            pool.wait_ge(s_pinit, 9)
            pool.wait_ge(s_mx, 1)
            pool.partition_all_reduce(stat[:, 6, 0:3], stat[:, 5, 0:3], P, RMAX).then_inc(s_mxa, 1)
            link = Chain(pool, pool_chain)

            def split_rows(a, z):
                for part in range(3):
                    link(pool.tensor_copy(bpart[:, a:z], bsum[:, a:z]))
                    link(pool.tensor_copy(bias[32 * part:32 * part + 1, a:z], bpart[32 * part:32 * part + 1, a:z]))
                    if part < 2:
                        link(pool.tensor_tensor(bsum[:, a:z], bsum[:, a:z], bpart[:, a:z], ALU.subtract))

            def scaled(x, i):
                link(pool.tensor_tensor(x, x, scl[:, i:i + 1].to_broadcast([P, x.shape[1]]), ALU.mult))

            pool.wait_ge(s_w[1], 16 * len(loads[1]))
            pool.wait_ge(s_prep, 1)
            for l in range(2):
                own = bsum[:, l * H:(l + 1) * H]
                link(pool.tensor_tensor(own, brec[:, 2 * l, :], brec[:, 2 * l + 1, :], ALU.add))
                scaled(own, l)
            split_rows(0, 2 * H)
            pool.tensor_copy(stat[:, 6, 7:8], stat[:, 6, 0:1]).then_inc(s_prep, 1)
            with pool.Fori(0, B) as b:
                norm_rstd(pool, b)

            def split3(parts, src, left):
                link(pool.tensor_copy(parts[0], src))
                link(pool.tensor_tensor(left, src, parts[0], ALU.subtract))
                link(pool.tensor_copy(parts[1], left))
                link(pool.tensor_tensor(left, left, parts[1], ALU.subtract))
                link(pool.tensor_copy(parts[2], left))

            pool.wait_ge(s_mx, 2)
            pool.partition_all_reduce(stat[:, 6, 0:6], stat[:, 5, 0:6], P, RMAX).then_inc(s_mxa, 1)
            pool.wait_ge(s_w[2], 16 * len(loads[2]))
            pool.wait_ge(s_prep, 4)
            for i in range(6):
                scaled(big[:, W_AT[i]:W_AT[i + 1]], S_FF1 + i)
            link(pool.tensor_copy(wx[0][:, :], big[:, :]))
            link(pool.tensor_tensor(wx[1][:, :], big[:, :], wx[0][:, :], ALU.subtract))
            scaled(bsum[:, B_V:B_V + D], S_V)
            split_rows(2 * H, 2 * H + 2 * D)
            split3([eb2p[:, i, :] for i in range(3)], eb2[:, :], rest[:, 0:D])
            link(pool.tensor_copy(sel16[:, :, :], self32[:, :, :]))
            link(pool.tensor_tensor(gate_bias[:, 0:NE], gate_bias[:, 0:NE], gate_bias[:, NE:2 * NE], ALU.add))
            with pool.Fori(0, T // BODY) as j:
                for q in range(2):
                    pool.wait_ge(s_h[1], j * BODY + (q + 1) * U)
                    pool.wait_ge(s_lo[1], OPEN + j * BODY + (q + 1) * U)
                    for k in range(KH):
                        for dst, src in ((all_hi, h_hi), (all_lo, h_lo)):
                            ins = pool.tensor_copy(dst[:, k, :, bass.ds(j * BODY + q * U, U)],
                                                   src[1][:, q, k, :, :].rearrange("p s b -> p b s"))
                    ins.then_inc(s_keep, 1)

            pool.wait_ge(s_keep, OPEN + T // U + 1)
            pool.wait_ge(s_lo[1], OPEN + T)
            pool.memset(cp[:, :, :], 0.0).then_inc(s_fcb, 1)
            with pool.Fori(0, 3 * B) as n:
                norm_rstd(pool, B + n)
            with pool.Fori(0, B) as b:
                norm_rstd(pool, 4 * B + b)
                pool.wait_ge(s_lg, b + 1)
                pool.tensor_tensor(gdiff[:, :, :, :], lg[:, :, :].unsqueeze(2).to_broadcast([P, TT, NE, NE]),
                                   lg[:, :, :].unsqueeze(3).to_broadcast([P, TT, NE, NE]),
                                   ALU.subtract).then_inc(s_rank, 1)

        @block.scalar
        def _(act):
            def table(function):
                act.activation(warm[:, :], nhalf[:, 0:1], function).then_inc(act_chain, 1)
                tables.append(function)
                act.wait_ge(act_chain, len(tables))

            tables = []
            act.wait_ge(s_pinit, 9)
            act.wait_ge(s_prep, 1)
            def load_scale(i):
                r = act.alloc_register(f"rescale{i}")
                act.reg_load(r, inv[0:1, i:i + 1].bitcast(I32))
                return r

            rescale = [load_scale(S_L0), load_scale(S_L1)]

            def rectify(b):
                for half in range(2):
                    act.wait_ge(s_conv, OPEN + b * 2 + half + 1)
                    act.wait_ge(s_proj, OPEN + b)
                    act.activation(relu[:, half, :], bank[half][:, :], ACT.Relu).then_inc(s_relu, 1)

            def time_major(b):
                norm_copy(act, xr[:, :, bass.ds(b, 1)].rearrange("p t b -> p (t b)"), bank[3], b)

            table(ACT.Tanh)
            rectify(0)
            with act.Fori(0, B - 1) as b:
                norm_square(act, b)
                rectify(b + 1)
                norm_high(act, b, b)
                time_major(b)
            norm_square(act, B - 1)
            norm_high(act, B - 1, B - 1)
            time_major(B - 1)
            recurrence(act, lambda e, g, j, l0, l1: rec_scalar(e, g, j, l0, l1, rescale))


            act.wait_ge(s_prep, 4)
            unscale = {i: load_scale(i) for i in (S_FF1, S_KQ1, S_V, S_E1)}
            act.wait_ge(s_w[2], 16 * len(loads[2]))
            table(ACT.Gelu_apprx_tanh)
            with act.Fori(0, B) as b:
                norm_square(act, B + b)
                norm_high(act, B + b, B + b)
                norm_copy(act, xt[:, bass.ds(b * T, T)], bank[1], B + b)
            act.wait_ge(s_wt, 1)
            act.activation(wt[0:NT, :], bank[6][0:NT, P:2 * P], ACT.Copy).then_inc(s_wtc, 1)

            with act.Fori(0, B) as b:
                act.wait_ge(s_y, OPEN + b)
                for half in range(2):
                    for m in range(KH):
                        act.wait_ge(s_ff, b * 4 + half * 2 + m + 1)
                        act.activation(gel[:, half, m, :], bank[2 + m][:, :], ACT.Gelu_apprx_tanh,
                                       bias=column(FF_B1 + m), scale=unscale[S_FF1]).then_inc(s_g, 1)
                act.wait_ge(s_y, OPEN + b + 1)
                act.wait_ge(s_yt, OPEN + b)
                act.activation(yt[:, :], bank[4][:, :], ACT.Identity, bias=column(FF_B2)).then_inc(s_yc, 1)

            table(ACT.Gelu)

            def front(b):
                norm_square(act, 2 * B + b)

            def last(b):
                norm_copy(act, xt[:, bass.ds(b * T, T)], bank[1], 2 * B + b)

            def back(b, more=True):
                for half in range(2):
                    if half:
                        act.wait_ge(s_v, b + 1)
                        act.activation(vv[:, span(b), :], tokens(bank[6][:, :]), ACT.Identity,
                                       scale=unscale[S_V]).then_inc(s_vr, 1)
                        if more:
                            norm_high(act, 2 * B + b + 1, 2 * B + b + 1)
                    act.wait_ge(s_kq, b * 2 + half + 1)
                    act.wait_ge(s_ph, OPEN + b * 2 + half)
                    act.activation(gel[:, half, 0, :], bank[2][:, :], ACT.Gelu, bias=column(KQ_B1),
                                   scale=unscale[S_KQ1]).then_inc(s_kqg, 1)
                    act.wait_ge(s_ph, OPEN + b * 2 + half + 1)
                    act.wait_ge(s_thr_r, OPEN + b * 2)
                    act.activation(th[:, half, :], bank[4][:, :], ACT.Tanh, bias=column(KQ_B2)).then_inc(s_th, 1)

            front(0)
            norm_high(act, 2 * B, 2 * B)
            last(0)
            with act.Fori(0, B - 1) as b:
                front(b + 1)
                back(b)
                last(b + 1)
            back(B - 1, False)

            act.wait_ge(s_thr_r, OPEN + 2 * B)
            table(ACT.Sin)

            sines = len(tables)

            def key_phasors(q, b):
                act.wait_ge(s_phi, b)
                act.activation(rabs[:, :], rph[:, bass.ds(b * T, T)], ACT.Abs).then_inc(act_chain, 1)
                act.wait_ge(act_chain, b + sines + 1)
                act.activation(phk[0:D, q, :], rabs[0:D, :], ACT.Sin, bias=col[0:D, QUARTER:QUARTER + 1], scale=-TWO_PI)
                act.activation(phk[D:P, q, :], rph[0:D, bass.ds(b * T, T)], ACT.Sin, scale=TWO_PI).then_inc(s_phk, 1)

            def query_phasors(q, b):
                act.activation(phq[0:D, q, :], rabs[D:P, :], ACT.Sin, bias=col[D:P, QUARTER:QUARTER + 1], scale=-TWO_PI)
                act.activation(phq[D:P, q, :], rph[D:P, bass.ds(b * T, T)], ACT.Sin, scale=TWO_PI).then_inc(s_phi, 1)

            def step(s, b):
                if 1 <= s:
                    norm_square(act, 3 * B + b - 1)
                if s < B - 1:
                    for half in range(2):
                        act.wait_ge(s_k, b * 2 + half + 3)
                        if s >= 0 and half == 0:
                            act.wait_ge(s_st, b + 1)
                        act.activation(kt[:, half * 4:half * 4 + 4, :].rearrange("p t k -> p (t k)"),
                                       bank[half][:, :], ACT.Copy).then_inc(s_kt, 1)
                if 0 <= s < B - 2:
                    act.wait_ge(s_s, b * 2 + 2)
                    key_phasors(s % 2, b + 2)
                if 1 <= s:
                    act.wait_ge(s_nt, b)
                    if s >= 2:
                        act.wait_ge(s_wo, b - 1)
                    act.activation(ntb[:, :], bank[6][:, :], ACT.Identity, bias=column(LN_B),
                                   scale=column(LN_W)).then_inc(s_ntc, 1)
                if 0 <= s < B - 2:
                    act.wait_ge(s_att, b + 1)
                    query_phasors(s % 2, b + 2)

            for b in range(2):
                key_phasors(b, b)
                query_phasors(b, b)
            attention(act, step)

            def gate_part(b, e):
                if e == 1:
                    norm_square(act, 4 * B + b)
                elif e == 3:
                    norm_high(act, 4 * B + b, 3 * B + b)
                elif e == 4:
                    norm_copy(act, xt[:, bass.ds(b * T, T)], bank[3], 3 * B + b)
                elif e == 6:
                    act.wait_ge(s_lm, OPEN + b + 1)
                    act.activation(gex[:, :, :], gc[:, :, :], ACT.Exp).then_inc(s_ex, 1)

            def weights(b):
                act.wait_ge(s_ct, OPEN + b + 1)
                act.wait_ge(s_c, OPEN + b * 16)
                act.activation(ct[:, :], bank[3].bitcast(F16)[:, 0:T], ACT.Copy).then_inc(s_ctc, 1)

            def expert(b, e):
                for half in range(2):
                    n = b * 16 + e * 2 + half
                    act.wait_ge(s_hid, n + 1)
                    act.wait_ge(s_gp, OPEN + b * 16 + max(0, e * 2 + half - 3))
                    act.activation(gr[:, e % 2, half, :], bank[4 + half][:, :], ACT.Relu,
                                   bias=ebias[:, e:e + 1], scale=unscale[S_E1]).then_inc(s_r, 1)

            def finish(b, more):
                act.wait_ge(s_moe, b + 1)
                act.wait_ge(s_moet, OPEN + b)
                act.activation(yt[:, :], bank[2][:, :], ACT.Copy).then_inc(s_moec, 1)

            act.activation(warm[:, :], nhalf[:, 0:1], ACT.Exp)
            experts(act, gate_part, weights, expert, finish, before=3)

        @block.tensor
        def _(pe):
            pe.wait_ge(s_w[0], 16 * len(loads[0]))
            pe.wait_ge(s_tabw, 1)
            for v in range(2):
                for tap in range(2):
                    mm = pe.matmul(bank[0][:, (v * 2 + tap) * P:(v * 2 + tap + 1) * P],
                                   embt[:, v * P:(v + 1) * P], wconv[:, tap, :], start=True, stop=True,
                                   skip_group_check=True)
            mm.then_inc(s_tab, 1)

            def convolve(b):
                pe.wait_ge(s_oh, b + 1)
                for half in range(2):
                    pe.wait_ge(s_relu, OPEN + b * 2 + half)
                    n = 0
                    for v in range(2):
                        for tap in range(2):
                            for part in range(3):
                                n += 1
                                mm = pe.matmul(bank[half][:, :], tab[part][:, v, tap, :],
                                               onehot[:, v, half * 512 + tap:half * 512 + tap + 512],
                                               start=(n == 1), stop=(n == 12))
                    mm.then_inc(s_conv, 1)

            def project0(b):
                pe.wait_ge(s_relu, OPEN + b * 2 + 2)
                pe.wait_ge(s_projr, OPEN + b)
                for t in range(TT):
                    mm = pe.matmul(bank[2][:, t * D:(t + 1) * D], relu[:, t // 4, (t % 4) * P:(t % 4 + 1) * P],
                                   wproj[:, :], start=True, stop=True, skip_group_check=True)
                mm.then_inc(s_proj, 1)

            convolve(0)
            pe.wait_ge(s_w[1], 16 * len(loads[1]))
            project0(0)
            with pe.Fori(0, B - 1) as b:
                convolve(b + 1)
                norm_turn(pe, bank[3], b)
                project0(b + 1)
            norm_turn(pe, bank[3], B - 1)
            pe.wait_ge(s_pinit, 9)
            pe.wait_ge(s_prep, 3)
            pe.wait_ge(s_xt, OPEN + B)
            for i in range(12):
                before0(pe, 0, 0, i)
            recurrence(pe, rec_tensor)
            pe.wait_ge(s_keep, OPEN + T // U + 1)
            pe.wait_ge(s_h[0], T)

            def fc(b):
                pe.wait_ge(s_fcr, OPEN + b)
                for t in range(TT):
                    n = 0
                    for w, h in ((wfc_hi, all_hi), (wfc_lo, all_hi), (wfc_hi, all_lo)):
                        for k in range(KH):
                            n += 1
                            states = h[:, k, :, :].rearrange("p b t -> p (b t)")
                            mm = pe.matmul(bank[0][:, t * D:(t + 1) * D],
                                           states[:, bass.ds(b * T + t * P, P)], w[:, k, :],
                                           start=(n == 1), stop=(n == 6), skip_group_check=True)
                mm.then_inc(s_fc, 1)

            def on_norm(dst, w0, width, b, half):
                for part in range(2):
                    mm = pe.matmul(dst, wx[part][:, w0:w0 + width], xt[:, bass.ds(b * T + half * 512, 512)],
                                   start=(part == 0), stop=(part == 1), skip_group_check=True)
                return mm

            def on_norm_tokens(bnk, w0, width, b, row=None):
                if row is not None:
                    row_bias(bnk, row)
                for t in range(TT):
                    for part in range(2):
                        mm = pe.matmul(bnk[:, t * width:(t + 1) * width], xt[:, bass.ds(b * T + t * P, P)],
                                       wx[part][:, w0:w0 + width], start=(row is None and part == 0),
                                       stop=(part == 1), skip_group_check=True)
                return mm

            def row_bias(bnk, at):
                pe.matmul(bnk[:, :].rearrange("p (t d) -> p t d", d=D), ones[:, :],
                          bias[:, at:at + D].unsqueeze(1).to_broadcast([P, TT, D]), start=True, stop=False,
                          skip_group_check=True)

            def router(b):
                pe.wait_ge(s_xt, OPEN + B + b + 1)
                for t in range(TT):
                    for part in range(2):
                        mm = pe.matmul(bank[6][:, bass.ds(b * TT + t, 1)], xt[:, bass.ds(b * T + t * P, P)],
                                       wx[part][:, W_WR:W_WR + 1], start=(part == 0), stop=(part == 1),
                                       skip_group_check=True)
                mm.then_inc(s_rw, 1)

            fc(0)
            with pe.Fori(0, B - 1) as b:
                fc(b + 1)
                norm_turn(pe, bank[1], B + b)
                router(b)
            norm_turn(pe, bank[1], 2 * B - 1)
            router(B - 1)
            pe.wait_ge(s_wr, 1)
            pe.transpose(bank[6][0:NT, P:2 * P], wr[:, :], eye[:, :]).then_inc(s_wt, 1)

            def ff(b):
                for half in range(2):
                    for m in range(KH):
                        pe.wait_ge(s_g, OPEN + b * 4 + max(0, half * 2 + m - 1))
                        on_norm(bank[2 + m][:, :], W_FF1 + m * P, P, b, half).then_inc(s_ff, 1)
                pe.wait_ge(s_g, OPEN + b * 4 + 4)
                pe.wait_ge(s_yc, OPEN + b)
                for m in range(KH):
                    for half in range(2):
                        mm = pe.matmul(bank[4][half * D:(half + 1) * D, :], ffw2[:, m, :], gel[:, half, m, :],
                                       start=(m == 0), stop=(m == KH - 1), skip_group_check=True)
                mm.then_inc(s_y, 1)
                pe.wait_ge(s_yc, OPEN + b + 1)
                pe.wait_ge(s_ytr, OPEN + b)
                for i in range(4):
                    mm = pe.transpose(bank[5][:, i * P:(i + 1) * P], yt[:, i * P:(i + 1) * P], eye[:, :])
                mm.then_inc(s_yt, 1)

            def count_digit(i):
                pe.wait_ge(s_enough, i + 1)
                pe.matmul(bank[0][:, 0:1], group[:, :], enough, start=True, stop=True).then_inc(s_digit, 1)

            ff(0)
            with pe.Fori(0, B - 1) as b:
                ff(b + 1)
                count_digit(b)
            count_digit(B - 1)
            pe.wait_ge(s_thr, 1)
            pe.matmul(bank[0][:, 0:B], ones32[:, :], thr8, start=True, stop=True).then_inc(s_thr_all, 1)
            pe.wait_ge(s_above, 1)
            pe.matmul(bank[0][:, 64:64 + B], ones32[:, :], sum8, start=True, stop=True, skip_group_check=True)
            pe.matmul(bank[0][:, 128:192], trix[:, :], equal, start=True, stop=True, skip_group_check=True)
            pe.matmul(bank[0][:, 192:256], ones32[:, :], equal, start=True, stop=True,
                      skip_group_check=True).then_inc(s_counted, 1)

            def kq(b):
                pe.wait_ge(s_xt, OPEN + 2 * B + b + 1)
                for half in range(2):
                    pe.wait_ge(s_kqg, OPEN + b * 2 + half)
                    on_norm(bank[2][:, :], W_KQ1, P, b, half).then_inc(s_kq, 1)
                    if half == 0:
                        pe.wait_ge(s_vr, OPEN + b)
                        on_norm_tokens(bank[6], W_V, D, b, B_V).then_inc(s_v, 1)
                    pe.wait_ge(s_kqg, OPEN + b * 2 + half + 1)
                    pe.wait_ge(s_th, OPEN + b * 2 + half)
                    pe.matmul(bank[4][:, :], wkq2[:, :], gel[:, half, 0, :], start=True, stop=True).then_inc(s_ph, 1)

            norm_turn(pe, bank[1], 2 * B)
            with pe.Fori(0, B - 1) as b:
                kq(b)
                norm_turn(pe, bank[1], 2 * B + b + 1)
            kq(B - 1)

            pe.wait_ge(s_vr, OPEN + B)

            def values(b, t):
                return vv[:, bass.ds(b * TT + t, 1), :].rearrange("p n d -> p (n d)")

            def scores(q, b, first):
                pe.wait_ge(s_phi, b + 1)
                for half in range(2):
                    if not first:
                        pe.wait_ge(s_kt, b * 2 + half - 1)
                    for i in range(4):
                        t = half * 4 + i
                        mm = pe.transpose(bank[half][:, i * P:(i + 1) * P], phk[:, q, t * P:(t + 1) * P], eye[:, :])
                    mm.then_inc(s_k, 1)
                for half in range(2):
                    if not first:
                        pe.wait_ge(s_sm, b * 2 + half - 1)
                    for i in range(4):
                        t = half * 4 + i
                        mm = pe.matmul(bank[2 + half][:, i * P:(i + 1) * P], phk[:, q, t * P:(t + 1) * P],
                                       phq[:, q, t * P:(t + 1) * P], start=True, stop=True, skip_group_check=True)
                    mm.then_inc(s_s, 1)

            def memory(b, first):
                pe.wait_ge(s_kt, b * 2 + 2)
                if not first:
                    pe.wait_ge(s_mem, b)
                for t in range(TT - 1):
                    mm = pe.matmul(bank[4][:, t * D:(t + 1) * D], kt[:, t, :], values(b, t), start=True, stop=True,
                                   skip_group_check=True)
                mm.then_inc(s_st, 1)

            def read(q, b, first):
                pe.wait_ge(s_sm, b * 2 + 2)
                pe.wait_ge(s_mem, b + 1)
                if not first:
                    pe.wait_ge(s_rt, b)
                for t in range(TT):
                    mm = pe.matmul(bank[5][:, t * D:(t + 1) * D], sm[:, q, t, :], values(b, t),
                                   start=True, stop=(t == 0), skip_group_check=True)
                    if t:
                        mm = pe.matmul(bank[5][:, t * D:(t + 1) * D], phq[:, q, t * P:(t + 1) * P], mem[:, t, :],
                                       start=False, stop=True, skip_group_check=True)
                mm.then_inc(s_att, 1)

            def step(s, b):
                if s < B - 1:
                    scores((s + 1) % 2, b + 1, s < 0)
                if 1 <= s:
                    pe.wait_ge(s_nrm, 3 * B + b)
                    for i in range(4):
                        mm = pe.transpose(bank[6][:, i * P:(i + 1) * P],
                                          nrm[:, 2 * i:2 * i + 2, :].rearrange("p t d -> p (t d)"), eye[:, :])
                    mm.then_inc(s_nt, 1)
                if 0 <= s < B:
                    read(s % 2, b, s == 0)
                if 1 <= s:
                    pe.wait_ge(s_ntc, b)
                    if s >= 2:
                        pe.wait_ge(s_wor, b - 1)
                    row_bias(bank[7], B_O)
                    for i in range(4):
                        mm = pe.matmul(bank[7][:, i * P:(i + 1) * P], ntb[:, i * P:(i + 1) * P], wobd[:, :],
                                       start=False, stop=True, skip_group_check=True)
                    mm.then_inc(s_wo, 1)
                if s < B - 1:
                    memory(b + 1, s < 0)

            attention(pe, step)

            pe.wait_ge(s_wor, B)

            def gate_part(b, e):
                if e == 3:
                    norm_turn(pe, bank[3], 3 * B + b)
                elif e == 4:
                    pe.wait_ge(s_xt, OPEN + 3 * B + b + 1)
                    pe.wait_ge(s_lm, OPEN + b)
                    on_norm_tokens(bank[0], W_G, NE, b).then_inc(s_gt, 1)

            def weights(b):
                pe.wait_ge(s_cp, b + 1)
                pe.wait_ge(s_xt, OPEN + 3 * B + b + 1)
                for t in range(TT):
                    mm = pe.transpose(bank[3].bitcast(F16)[:, t * P:(t + 1) * P], cp[:, t, :], eye16[:, :])
                mm.then_inc(s_ct, 1)
                if isinstance(b, int):
                    hidden(b, 0, 0)
                    hidden(b, 0, 1)

            def second(b, e):
                for half in range(2):
                    pe.wait_ge(s_gp, OPEN + b * 16 + e * 2 + half + 1)
                    mm = pe.matmul(bank[2][half * D:(half + 1) * D, :], ew2[:, e, :], gp[:, e % 2, half, :],
                                   start=False, stop=(e == NE - 1), skip_group_check=True)
                return mm

            def hidden(b, e, half):
                pe.wait_ge(s_r, OPEN + b * 16 + max(0, e * 2 + half - 1))
                on_norm(bank[4 + half][:, :], W_E1 + e * HE, HE, b, half).then_inc(s_hid, 1)

            def weight(b, e, half):
                pe.wait_ge(s_gp, OPEN + b * 16 + max(0, e * 2 + half - 1))
                pe.matmul(bank[6 + half][:, :], sel16[:, e, :], ct[:, half * 512:(half + 1) * 512],
                          start=True, stop=True).then_inc(s_c, 1)

            def expert(b, e):
                if e == 0:
                    pe.wait_ge(s_ctc, b + 1)
                    weight(b, e, 0)
                    weight(b, e, 1)
                    pe.wait_ge(s_moec, OPEN + b)
                    for part in range(3):
                        for half in range(2):
                            pe.matmul(bank[2][half * D:(half + 1) * D, :], eb2p[:, part, :],
                                      ct[:, half * 512:(half + 1) * 512], start=(part == 0), stop=False,
                                      skip_group_check=True)
                else:
                    for half in range(2):
                        hidden(b, e, half)
                        weight(b, e, half)
                    second(b, e - 1)

            def finish(b, more):
                second(b, NE - 1).then_inc(s_moe, 1)
                if more:
                    hidden(b + 1, 0, 0)
                    hidden(b + 1, 0, 1)
                pe.wait_ge(s_moec, OPEN + b + 1)
                pe.wait_ge(s_fin, OPEN + b)
                for i in range(4):
                    mm = pe.transpose(bank[1][:, i * P:(i + 1) * P], yt[:, i * P:(i + 1) * P], eye[:, :])
                mm.then_inc(s_moet, 1)

            experts(pe, gate_part, weights, expert, finish)

        @block.vector
        def _(dve):
            link = Chain(dve, dve_chain)

            def split3(parts, src, left):
                link(dve.tensor_copy(parts[0], src))
                link(dve.tensor_tensor(left, src, parts[0], ALU.subtract))
                link(dve.tensor_copy(parts[1], left))
                link(dve.tensor_tensor(left, left, parts[1], ALU.subtract))
                link(dve.tensor_copy(parts[2], left))

            dve.wait_ge(s_w[0], 16 * len(loads[0]))
            dve.memset(embt[:, 0:1], 0.0).then_inc(s_tabw, 1)
            dve.wait_ge(s_pinit, 9)
            dve.wait_ge(s_w[1], 16 * len(loads[1]))
            link(dve.tensor_reduce(stat[:, 0, 0:1], wih0[:, :], AX.X, ALU.max, apply_absolute_value=True))
            for i in range(3):
                link(dve.tensor_reduce(stat[:, 0, i + 1:i + 2], wrec[:, i, :, :], AX.XY, ALU.max,
                                       apply_absolute_value=True))
            link(dve.tensor_reduce(stat[:, 5, 2:3], wfc[:, :, :], AX.XY, ALU.max, apply_absolute_value=True))
            link(dve.tensor_tensor(stat[:, 5, 0:1], stat[:, 0, 0:1], stat[:, 0, 1:2], ALU.max))
            dve.tensor_tensor(stat[:, 5, 1:2], stat[:, 0, 2:3], stat[:, 0, 3:4], ALU.max).then_inc(s_mx, 1)
            dve.wait_ge(s_tab, 1)
            split3([t[:, :, :, :].rearrange("p a b c -> p (a b c)") for t in tab], bank[0][:, :], left512[:, :])
            def scales(a, z, turn):
                n = z - a
                dve.wait_ge(s_mxa, turn)
                link(dve.tensor_scalar(stat[:, 7, 0:n], stat[:, 6, 0:n], 2.0 ** -100, None, ALU.max))
                link(dve.tensor_scalar(stat[:, 0, 0:n].bitcast(I32), stat[:, 7, 0:n].bitcast(I32),
                                       0x7F800000, None, ALU.bitwise_and))
                link(dve.reciprocal(stat[:, 1, 0:n], stat[:, 0, 0:n]))
                link(dve.tensor_scalar(scl[:, a:z], stat[:, 1, 0:n], 2.0 ** 13, None, ALU.mult))
                dve.tensor_scalar(inv[:, a:z], stat[:, 0, 0:n], 2.0 ** -13, None, ALU.mult).then_inc(s_prep, 1)

            scales(0, 3, 1)

            def one_hot(b):
                dve.wait_ge(s_conv, OPEN + b * 2)
                for v in range(2):
                    ins = dve.tensor_scalar(onehot[:, v, 1:T + 1], ids[:, bass.ds(b, 1), :].rearrange(
                        "p b t -> p (b t)"), vid[:, v:v + 1], None, ALU.is_equal)
                ins.then_inc(s_oh, 1)

            def norms(b):
                dve.wait_ge(s_xs, OPEN + b)
                dve.wait_ge(s_proj, OPEN + b + 1)
                dve.tensor_tensor(cur[:, :, :], tokens(bank[2][:, :]), rows(bproj[:, :]), ALU.add).then_inc(s_projr, 1)
                dve.wait_ge(s_projr, OPEN + b + 1)
                norm_centre(dve, link)
                dve.tensor_tensor(res[:, bass.ds(b * TT, TT), :], cur[:, :, :], rows(fcb[:, :]), ALU.add)
                norm_variance(dve, link, b)
                norm_scale(dve, b)
                norm_low(dve, b)

            for i in range(4):
                dve.wait_ge(s_ids[i], 16)
            one_hot(0)
            for i, (hi, lo, s) in enumerate(((whh_hi[0], whh_lo[0], 0), (wih1_hi, wih1_lo, 1),
                                             (whh_hi[1], whh_lo[1], 1))):
                link(dve.tensor_scalar(hi[:, :, :], wrec[:, i, :, :], scl[:, s:s + 1], None, ALU.mult))
                link(dve.scalar_tensor_tensor(lo[:, :, :], wrec[:, i, :, :], scl[:, s:s + 1], hi[:, :, :],
                                              ALU.mult, ALU.subtract))
            link(dve.tensor_scalar(wih0_hi[:, :], wih0[:, :], scl[:, 0:1], None, ALU.mult))
            link(dve.scalar_tensor_tensor(wih0_lo[:, :], wih0[:, :], scl[:, 0:1], wih0_hi[:, :], ALU.mult, ALU.subtract))
            link(dve.tensor_scalar(wfc_hi[:, :, :], wfc[:, :, :], scl[:, 2:3], None, ALU.mult))
            dve.scalar_tensor_tensor(wfc_lo[:, :, :], wfc[:, :, :], scl[:, 2:3], wfc_hi[:, :, :],
                                     ALU.mult, ALU.subtract).then_inc(s_prep, 1)
            with dve.Fori(0, B - 1) as b:
                link.loop(b, 3)
                one_hot(b + 1)
                norms(b)
                link.end(B - 1)
            norms(B - 1)
            dve.wait_ge(s_w[2], 16 * len(loads[2]))
            for i in range(6):
                link(dve.tensor_reduce(stat[:, 5, i:i + 1], big[:, W_AT[i]:W_AT[i + 1]], AX.X, ALU.max,
                                       apply_absolute_value=True))
            dve.tensor_copy(stat[:, 5, 6:7], stat[:, 5, 0:1]).then_inc(s_mx, 1)
            scales(S_FF1, S_END, 2)
            recurrence(dve, rec_vector)

            def halves(x):
                return x.rearrange("p (i h d) -> p h i d", i=4, h=2)

            def front(b):
                dve.wait_ge(s_xs, OPEN + B + b)
                dve.wait_ge(s_fc, b + 1)
                dve.scalar_tensor_tensor(cur[:, :, :], tokens(bank[0][:, :]), inv[:, 2:3], res[:, span(b), :],
                                         ALU.mult, ALU.add).then_inc(s_fcr, 1)
                dve.wait_ge(s_fcr, OPEN + b + 1)
                norm_vector(dve, link, B + b)
                dve.tensor_tensor(res[:, span(b), :], cur[:, :, :], nrm[:, :, :], ALU.add)
                norm_low(dve, B + b)

            dve.wait_ge(s_fcb, 1)
            with dve.Fori(0, B) as b:
                link.loop(b, 3)
                front(b)
                link.end(B)
            dve.wait_ge(s_rw, B)
            dve.tensor_scalar(wr[:, :], bank[6][:, 0:NT], inv[:, S_WR:S_WR + 1], column(WR_B), ALU.mult, ALU.add).then_inc(s_wr, 1)
            dve.wait_ge(s_wr, 1)

            def to_float(src):
                link(dve.tensor_scalar(flip, src, 31, -1, ALU.arith_shift_right, ALU.bitwise_xor))
                link(dve.scalar_tensor_tensor(fbits, flip, -2 ** 31, src, ALU.bitwise_or, ALU.bitwise_xor))

            link(dve.memset(key, 0))
            for b in range(B):
                dve.wait_ge(s_yt, OPEN + b + 1)
                dve.tensor_tensor(yw[:, b * TT:(b + 1) * TT, :].rearrange("p (h i) d -> p h i d", h=2),
                                  halves(bank[5][:, :]),
                                  wr[:, b * TT:(b + 1) * TT].rearrange("p (h i) -> p h i", h=2).unsqueeze(
                                      3).to_broadcast([P, 2, 4, D]), ALU.mult).then_inc(s_ytr, 1)
                if b == 0:
                    dve.wait_ge(s_wall, 16 * B)
                shift = 28 - 4 * b
                link(dve.tensor_tensor(cand, key, digit[:, b:b + 1], ALU.bitwise_or))
                to_float(cand)
                link(dve.tensor_scalar(junk, wall, fbits.bitcast(F32), 0.0, ALU.is_ge, ALU.add, accum_out=cnt))
                dve.tensor_scalar(enough, cnt, KEEP - 0.5, None, ALU.is_ge).then_inc(s_enough, 1)
                dve.wait_ge(s_digit, b + 1)
                link(dve.tensor_copy(digi, bank[0][:, 0:1]))
                if shift:
                    link(dve.tensor_scalar(digi, digi, shift, None, ALU.logical_shift_left))
                link(dve.tensor_tensor(key, key, digi, ALU.bitwise_or))
            to_float(key)
            dve.tensor_scalar(thr8, first8[:, :], fbits.bitcast(F32), None, ALU.mult).then_inc(s_thr, 1)
            dve.wait_ge(s_thr_all, 1)
            by_seq = lambda x: x.rearrange("p (b t) -> p b t", b=B)
            over = lambda x: x.unsqueeze(2).to_broadcast([P, B, TT])
            link(dve.tensor_tensor(by_seq(above), by_seq(wr[:, :]), over(bank[0][:, 0:B]), ALU.is_gt))
            link(dve.tensor_tensor(by_seq(equal), by_seq(wr[:, :]), over(bank[0][:, 0:B]), ALU.is_equal))
            dve.reduce_sum(sum8, by_seq(above), AX.X).then_inc(s_above, 1)
            dve.wait_ge(s_counted, 1)
            link(dve.tensor_scalar(sum8, bank[0][:, 64:64 + B], -1.0, float(KEEP), ALU.mult, ALU.add))
            link(dve.memset(by_seq(offs)[:, :, 0:1], 0.0))
            for t in range(1, TT):
                link(dve.tensor_tensor(by_seq(offs)[:, :, t:t + 1], by_seq(offs)[:, :, t - 1:t],
                                       by_seq(bank[0][:, 192:256])[:, :, t - 1:t], ALU.add))
            link(dve.tensor_tensor(before, offs, bank[0][:, 128:192], ALU.add))
            link(dve.tensor_tensor(by_seq(before), by_seq(before), over(sum8), ALU.is_lt))
            link(dve.tensor_tensor(before, before, equal, ALU.mult))
            link(dve.tensor_tensor(pick[:, :], before, above, ALU.add))

            def front(b):
                dve.wait_ge(s_xs, OPEN + 2 * B + b)
                link(dve.tensor_tensor(tmp8[:, :, :], yw[:, span(b), :], spread(pick[:, span(b)]), ALU.mult))
                link(dve.tensor_tensor(cur[:, :, :], tmp8[:, :, :], res[:, span(b), :], ALU.add))
                norm_vector(dve, link, 2 * B + b)
                dve.tensor_tensor(res[:, span(b), :], cur[:, :, :], nrm[:, :, :], ALU.add)
                norm_low(dve, 2 * B + b)

            def back(b):
                for half in range(2):
                    dve.wait_ge(s_thr_r, OPEN + b * 2 + half)
                    dve.wait_ge(s_th, OPEN + b * 2 + half + 1)
                    link(dve.tensor_scalar(turns[:, :], th[:, half, :], column(TURNS), None, ALU.mult))
                    link(dve.tensor_scalar(whole[:, :], turns[:, :], MAGIC, -MAGIC, ALU.add, ALU.add))
                    dve.tensor_tensor(rph[:, bass.ds(b * T + half * 512, 512)], turns[:, :], whole[:, :],
                                      ALU.subtract).then_inc(s_thr_r, 1)

            skewed(dve, front, back, link, 9)

            def step(s, b):
                if 1 <= s:
                    dve.wait_ge(s_att, b)
                    dve.tensor_tensor(cur[:, :, :], tokens(bank[5][:, :]), spread(posr[:, :]), ALU.mult).then_inc(s_rt, 1)
                    dve.wait_ge(s_rt, b)
                    norm_centre(dve, link)
                if 0 <= s < B:
                    dve.wait_ge(s_st, b + 1)
                    link(dve.tensor_copy(mem[:, 1, :], bank[4][:, 0:D]))
                    for t in range(2, TT):
                        ins = dve.tensor_tensor(mem[:, t, :], mem[:, t - 1, :], bank[4][:, (t - 1) * D:t * D], ALU.add)
                        if t < TT - 1:
                            link(ins)
                    ins.then_inc(s_mem, 1)
                if 1 <= s:
                    norm_variance(dve, link, 3 * B + b - 1)
                    norm_scale(dve, 3 * B + b - 1)
                if s < B - 1:
                    for half in range(2):
                        dve.wait_ge(s_s, b * 2 + half + 3)
                        dve.tensor_tensor(sm[:, (s + 1) % 2, half * 4:half * 4 + 4, :],
                                          bank[2 + half][:, :].rearrange("p (t k) -> p t k", t=4),
                                          tri[:, :].unsqueeze(1).to_broadcast([P, 4, P]), ALU.mult).then_inc(s_sm, 1)
                if 1 <= s:
                    dve.wait_ge(s_wo, b)
                    dve.tensor_tensor(res[:, span(b - 1), :], tokens(bank[7][:, :]), res[:, span(b - 1), :],
                                      ALU.add).then_inc(s_wor, 1)

            attention(dve, step, link, 18)
            dve.wait_ge(s_wor, B)

            per = lambda x: x.unsqueeze(2).to_broadcast([P, TT, NE])
            k = 4 * B

            def gate_part(b, e):
                if e == 0:
                    dve.wait_ge(s_nrm, k + b)
                    link(dve.tensor_scalar(cur[:, :, :], res[:, span(b), :], 1.0, None, ALU.mult))
                    norm_centre(dve, link)
                elif e == 1:
                    norm_variance(dve, link, k + b)
                elif e == 2:
                    norm_scale(dve, k + b)
                elif e == 3:
                    norm_low(dve, 3 * B + b)
                elif e == 5:
                    dve.wait_ge(s_gt, b + 1)
                    dve.scalar_tensor_tensor(lg[:, :, :], bank[0][:, 0:TT * NE].rearrange(
                        "p (t e) -> p t e", t=TT), inv[:, S_G:S_G + 1],
                        gate_bias[:, 0:NE].unsqueeze(1).to_broadcast([P, TT, NE]), ALU.mult, ALU.add).then_inc(s_lg, 1)
                    dve.wait_ge(s_lg, b + 1)
                    link(dve.tensor_reduce(stat[:, 5, :], lg[:, :, :], AX.X, ALU.max))
                    dve.tensor_tensor(gc[:, :, :], lg[:, :, :], per(stat[:, 5, :]), ALU.subtract).then_inc(s_lm, 1)
                elif e == 6:
                    dve.wait_ge(s_rank, b + 1)
                    link(dve.tensor_tensor(gdiff[:, :, :, :], gdiff[:, :, :, :],
                                           order[:, :, :].unsqueeze(1).to_broadcast([P, TT, NE, NE]), ALU.is_gt))
                elif e == 7:
                    link(dve.reduce_sum(grank[:, :, :], gdiff[:, :, :, :], AX.X))
                    link(dve.tensor_scalar(gsel[:, :, :], grank[:, :, :], 1.5, None, ALU.is_lt))
                    dve.wait_ge(s_ex, b + 1)
                    link(dve.tensor_tensor(gc[:, :, :], gex[:, :, :], gsel[:, :, :], ALU.mult))
                    link(dve.reduce_sum(stat[:, 6, :], gc[:, :, :], AX.X))
                    link(dve.reciprocal(stat[:, 7, :], stat[:, 6, :]))
                    link(dve.tensor_tensor(gleft[:, :, :], gc[:, :, :], per(stat[:, 7, :]), ALU.mult))
                    dve.wait_ge(s_ct, OPEN + b)
                    link(dve.tensor_copy(cp[:, :, 0:NE], gleft[:, :, :]))
                    dve.tensor_tensor(cp[:, :, NE:2 * NE], gleft[:, :, :], cp[:, :, 0:NE],
                                      ALU.subtract).then_inc(s_cp, 1)

            def expert(b, e):
                for half in range(2):
                    n = b * 16 + e * 2 + half
                    dve.wait_ge(s_r, OPEN + n + 1)
                    dve.wait_ge(s_c, OPEN + n + 1)
                    dve.tensor_tensor(gp[:, e % 2, half, :], gr[:, e % 2, half, :], bank[6 + half][:, :],
                                      ALU.mult).then_inc(s_gp, 1)

            def finish(b, more):
                dve.wait_ge(s_moet, OPEN + b + 1)
                own = res[:, span(b), :].rearrange("p (h i) d -> p h i d", h=2)
                dve.tensor_tensor(own, halves(bank[1][:, :]), own, ALU.add).then_inc(s_fin, 1)

            experts(dve, gate_part, lambda b: None, expert, finish, link, 13, before=3)


def lay_out(inp):
    f = lambda n: np.ascontiguousarray(inp[n])
    twice = lambda w: np.concatenate([w, w], 0)
    conv = f("L0_tok_conv_w")
    wconv = np.zeros((P, 2, P), conv.dtype)
    for g in range(P // 8):
        for tap in range(2):
            wconv[g * 8:g * 8 + 8, tap, g * 8:g * 8 + 8] = conv[g * 8:g * 8 + 8, :, tap].T
    tiles = lambda w: w.T.reshape(KH, P, -1).transpose(1, 0, 2)
    wx = np.concatenate([
        f("L0_ffn_w1"), f("L1_attn_Wk1"), f("L1_attn_Wq1"), f("L1_attn_Wv"), f("L1_ffn_Wg"),
        f("L1_ffn_W1").transpose(1, 0, 2).reshape(D, NE * HE), f("L0_ffn_wr")], 1)
    z = lambda *shape: np.zeros(shape, np.float32)
    col = z(P, 16)
    col[:, 0:2] = f("L0_ffn_b1").reshape(KH, P).T
    for i, (k, q) in ((2, ("bk1", "bq1")), (3, ("bk2", "bq2")), (4, ("ln_w", "ln_w")), (5, ("ln_b", "ln_b"))):
        col[:D, i], col[D:, i] = f("L1_attn_" + k), f("L1_attn_" + q)
    col[:, 6] = np.pi / 2
    col[:, 7] = f("L0_ffn_br")[0]
    col[:, 8] = np.tile(np.repeat(2.0 ** np.arange(4), 16), 2) / 2
    col[:, 9] = np.tile(f("L0_ffn_b2"), 2)
    wkq2, wobd = z(P, P), z(P, P)
    wkq2[:D, :D], wkq2[D:, D:] = f("L1_attn_Wk2"), f("L1_attn_Wq2")
    wobd[:D, :D] = wobd[D:, D:] = f("L1_attn_Wo")
    eb2, select = z(P, D), z(P, NE, P)
    for part in range(2):
        eb2[part * NE:part * NE + NE] = f("L1_ffn_b2")
        for e in range(NE):
            select[part * NE + e, e] = 1
    p = np.arange(P)
    group = ((p[:, None] // 16 == p // 16) & (p[:, None] % 16 > 0)).astype(np.float32)
    first8 = (p[:, None] == 16 * np.arange(B)).astype(np.float32)
    digit = ((p[:, None] % 16).astype(np.int64) << (28 - 4 * np.arange(8))).astype(np.uint32).view(np.int32)
    digit[::16, 0] = -2 ** 31
    posr = (1.0 / np.sqrt((p[:, None] + P * np.arange(TT) + 1.0) * D)).astype(np.float32)
    e = np.arange(NE)
    order = np.where(e < e[:, None], -1e-37, np.where(e == e[:, None], 1.0, 0.0)).astype(np.float32)
    a = {
        "x": f("x"),
        "wx": twice(wx), "wih0": twice(f("L0_attn_W_ih_0").T),
        "wrec": np.stack([tiles(f(n)) for n in ("L0_attn_W_hh_0", "L0_attn_W_ih_1", "L0_attn_W_hh_1")], 1),
        "wfc": tiles(f("L0_attn_fc_w")),
        "brec": np.concatenate([f(n) for n in ("L0_attn_b_ih_0", "L0_attn_b_hh_0", "L0_attn_b_ih_1",
                                               "L0_attn_b_hh_1")]),
        "embt": f("L0_tok_embed_table").T,
        "wconv": wconv,
        "wproj": f("L0_tok_proj_w").T,
        "proj_b": f("L0_tok_proj_b"),
        "fc_b": f("L0_attn_fc_b"),
        "bov": np.concatenate([f("L1_attn_bo"), f("L1_attn_bv")]),
        "gb": np.concatenate([f("L1_ffn_bg"), f("L1_ffn_bias")]),
        "col": col, "ebias": f("L1_ffn_b1").T, "ffw2": f("L0_ffn_w2").reshape(KH, P, D).transpose(1, 0, 2),
        "wkq2": wkq2, "wobd": wobd, "ew2": f("L1_ffn_W2").transpose(1, 0, 2), "eb2": eb2, "self32": select,
        "tri": np.triu(np.ones((P, P), np.float32)), "trix": np.triu(np.ones((P, P), np.float32), 1),
        "group": group, "first8": first8, "digit": digit,
        "posr": posr, "order": np.broadcast_to(order, (P, NE, NE)),
        "vid": np.arange(VOC, dtype=np.float32).reshape(2, P).T,
        "eye": np.eye(P, dtype=np.float32),
        "eye16": np.eye(P, dtype=np.float16),
    }
    return {k: np.ascontiguousarray(v) for k, v in a.items()}


def kernel(**inputs):
    import concourse.bacc as bacc
    from concourse.bass_utils import run_bass_kernel_spmd

    nc = bacc.Bacc("TRN2", target_bir_lowering=False, num_devices=1)
    arrays = {f"in_{k}": v for k, v in lay_out(inputs).items()}
    args = {k[3:]: nc.dram_tensor(k, v.shape, mybir.dt.from_np(v.dtype), kind="ExternalInput").ap()
            for k, v in arrays.items()}
    out = nc.dram_tensor("out", (B, T, D), F32, kind="ExternalOutput").ap()
    build(nc, args, out)
    r = run_bass_kernel_spmd(nc, [arrays], core_ids=[0])
    return r.results[0]["out"]
```
